# Optimizing a Trainium2 kernel written in Bass

```python
import numpy as np
import jax
import jax.numpy as jnp

def _softmax(x, axis=-1):
    return jax.nn.softmax(x, axis=axis)

def _gelu(x):
    return jax.nn.gelu(x, approximate=True)

def _silu(x):
    return jax.nn.silu(x)

def _sigmoid(x):
    return jax.nn.sigmoid(x)

def _layernorm(x, axis=-1, eps=1e-05):
    m = jnp.mean(x, axis=axis, keepdims=True)
    v = jnp.var(x, axis=axis, keepdims=True)
    return (x - m) / jnp.sqrt(v + eps)

def _scatter_add(tgt, idx, src, axis=0):
    return tgt.at[idx].add(src)

def _segment_sum(src, seg, n):
    return jax.ops.segment_sum(src, seg, n)
kernel_name = 'mk_gnn_resnorm_d1_gnn_r64_caf647'

def setup_inputs(seed: int=0):
    np.random.seed(seed)
    _w = jnp.asarray

    def _rec_inputs():
        import jax
        import jax.numpy as jnp
        _gk = jax.random.key(seed)
        x = -0.0007083 + 1.001 * jax.random.normal(jax.random.fold_in(_gk, 1), (100000, 48), jnp.float32)
        src = jax.random.randint(jax.random.fold_in(_gk, 2), (25000,), 0, 100000, jnp.int32)
        dst = jax.random.randint(jax.random.fold_in(_gk, 3), (25000,), 0, 100000, jnp.int32)
        _o = jnp.argsort(dst, stable=True)
        src = src[_o]
        dst = dst[_o]
        edge_attr_40 = jax.random.uniform(jax.random.fold_in(_gk, 12), (25000, 40), jnp.float32, 0.0, 1)
        edge_weight = jax.random.uniform(jax.random.fold_in(_gk, 14), (25000,), jnp.float32, 0.0, 6.99999)
        node_type_119 = jax.random.randint(jax.random.fold_in(_gk, 15), (100000,), 0, 119, jnp.int32)
        node_vec = jax.random.uniform(jax.random.fold_in(_gk, 16), (100000,), jnp.float32, 0.0, 1.49999)
        return (x, src, dst, edge_attr_40, edge_weight, node_type_119, node_vec)
    x, src, dst, edge_attr_40, edge_weight, node_type_119, node_vec = _rec_inputs()

    def _L0_gnn_setup():
        import jax, jax.numpy as jnp
        import numpy as np
        CUTOFF = 6.0
        LN_EPS = 1e-05
        key = jax.random.key(seed)
        ks = jax.random.split(key, 16)
        N, E, H, R, NEL, G = (50000, 12500, 48, 40, 119, 32)
        inp = {'h': jax.random.normal(ks[0], (N, H), jnp.float32), 'edge_index': jax.random.randint(ks[1], (2, E), 0, N, jnp.int64), 'edge_attr': jax.random.uniform(ks[2], (E, R), jnp.float32), 'distances': jax.random.uniform(ks[3], (E,), jnp.float32) * 7.0, 'atom_z': jax.random.randint(ks[4], (N,), 0, NEL, jnp.int64), 'node_mult': jax.random.uniform(ks[5], (N,), jnp.float32) + 0.5, 'batch': jnp.zeros((N,), jnp.int64), 'W1': jax.random.normal(ks[6], (H, R), jnp.float32) / np.sqrt(R), 'b1': jax.random.normal(ks[7], (H,), jnp.float32) * 0.01, 'W2': jax.random.normal(ks[8], (H, H), jnp.float32) / np.sqrt(H), 'b2': jax.random.normal(ks[9], (H,), jnp.float32) * 0.01, 'emb': jax.random.normal(ks[10], (NEL, G), jnp.float32) * 0.01, 'adaptW': jax.random.normal(ks[11], (G, G), jnp.float32) * 0.01, 'gamma': jnp.ones((H,), jnp.float32), 'beta': jnp.zeros((H,), jnp.float32)}
        return inp
    _L0_gnn_all = _L0_gnn_setup()
    _L0_gnn_in = {k: v for k, v in _L0_gnn_all.items() if k in ('W1', 'b1', 'W2', 'b2', 'emb', 'adaptW', 'gamma', 'beta')}
    del _L0_gnn_all
    return {'x': x, 'src': src, 'dst': dst, 'edge_attr_40': edge_attr_40, 'edge_weight': edge_weight, 'node_type_119': node_type_119, 'node_vec': node_vec, 'L0_gnn_W1': _L0_gnn_in['W1'], 'L0_gnn_b1': _L0_gnn_in['b1'], 'L0_gnn_W2': _L0_gnn_in['W2'], 'L0_gnn_b2': _L0_gnn_in['b2'], 'L0_gnn_emb': _L0_gnn_in['emb'], 'L0_gnn_adaptW': _L0_gnn_in['adaptW'], 'L0_gnn_gamma': _L0_gnn_in['gamma'], 'L0_gnn_beta': _L0_gnn_in['beta']}

def reference(x, src, dst, edge_attr_40, edge_weight, node_type_119, node_vec, L0_gnn_W1, L0_gnn_b1, L0_gnn_W2, L0_gnn_b2, L0_gnn_emb, L0_gnn_adaptW, L0_gnn_gamma, L0_gnn_beta):
    import jax
    import jax.numpy as jnp

    def _L0_gnn_ref(h, edge_index, edge_attr, distances, atom_z, node_mult, batch, W1, b1, W2, b2, emb, adaptW, gamma, beta):
        import jax, jax.numpy as jnp
        import numpy as np
        CUTOFF = 6.0
        LN_EPS = 1e-05
        src, dst = (edge_index[0], edge_index[1])
        N = h.shape[0]
        gate = jax.nn.silu(edge_attr @ W1.T + b1) @ W2.T + b2
        ei = emb[atom_z[src]]
        ej = emb[atom_z[dst]]
        adapt_logit = jnp.sum(ei * (ej @ adaptW.T), axis=-1, keepdims=True)
        gate = gate + adapt_logit
        cw = jnp.where(distances < CUTOFF, 0.5 * (jnp.cos(jnp.pi * distances / CUTOFF) + 1.0), 0.0)
        mj = node_mult[dst]
        msg = gate * h[dst] * (cw * mj)[:, None]
        agg = jax.ops.segment_sum(msg, src, num_segments=N)
        tot = jax.ops.segment_sum(mj, src, num_segments=N)
        agg = agg / jnp.clip(tot, 1e-08, None)[:, None]
        x = h + agg
        mu = jnp.mean(x, axis=-1, keepdims=True)
        var = jnp.mean(jnp.square(x - mu), axis=-1, keepdims=True)
        return (x - mu) / jnp.sqrt(var + LN_EPS) * gamma + beta
    edge_index = jnp.stack([src, dst])
    batch0 = jnp.zeros((100000,), jnp.int32)
    x = _layernorm(x + _L0_gnn_ref(x, edge_index, edge_attr_40, edge_weight, node_type_119, node_vec, batch0, L0_gnn_W1, L0_gnn_b1, L0_gnn_W2, L0_gnn_b2, L0_gnn_emb, L0_gnn_adaptW, L0_gnn_gamma, L0_gnn_beta), axis=-1)
    return x

_drawn_inputs = setup_inputs


def setup_inputs(seed=0):
    import zlib

    import numpy as np

    out = dict(_drawn_inputs(seed))
    spreads = {'L0_gnn_gamma': (1.0, 0.2), 'L0_gnn_beta': (0.0, 0.1)}
    factors = {'node_vec': 64.0,
     'L0_gnn_b1': 64.0,
     'L0_gnn_b2': 45.691,
     'L0_gnn_emb': 64.0,
     'L0_gnn_adaptW': 64.0}
    for name, (base, spread) in spreads.items():
        noise = np.random.default_rng([zlib.crc32(name.encode()), seed]).standard_normal(out[name].shape)
        drawn = base * np.exp(spread * noise) if base else spread * noise
        out[name] = jnp.asarray(drawn.astype(out[name].dtype))
    for name, factor in factors.items():
        out[name] = (out[name] * factor).astype(out[name].dtype)
    return out
```

```python
from contextlib import ExitStack

import concourse.bass as bass
from concourse import mybir

ALU = mybir.AluOpType
ACT = mybir.ActivationFunctionType
BF16 = mybir.dt.bfloat16
F32 = mybir.dt.float32
I32 = mybir.dt.int32
AX_X = mybir.AxisListType.X

P = 128
N = 100000
H = 48
E = 25000
R_ATTR = 40
NZ = 119
G = 32
CUTOFF = 6.0
EPS = 1e-5
TOT_MIN = 1e-8

C = 4
EC = C * P
NCH = -(-E // EC)
EPAD = NCH * EC
NT = NCH * C
RING = 4
PEEL = RING + 1
assert (NCH - PEEL) % RING == 0

W = H + 2
S = H + 1
TRASH = N
PAD_ROW = N + 2 * P
SUM_J = 784
SUM_ROWS = P * SUM_J
CLEAR_J = 28
CLEAR_REP = 4
assert SUM_ROWS > PAD_ROW and SUM_J % (CLEAR_J * CLEAR_REP) == 0

NJ = N // P
REST = N - NJ * P
XJ = NJ + 1
CJ = 17
NST = XJ // CJ
assert NST * CJ == XJ
X_PARTS = 4


def gnn_resnorm(nc, x, table, src_row, cols, src_col, weight, attr, node_z, w1, b1, w2, b2, emb_t, adapt_t,
                gamma, beta, out):
    sums = nc.dram_tensor("sums", (SUM_ROWS, S), F32, kind="Internal").ap()
    ctx = ExitStack()
    with ctx:
        def sb(name, shape, dt):
            return ctx.enter_context(nc.sbuf_tensor(name, shape, dt))

        def sem(name):
            return ctx.enter_context(nc.semaphore(name))

        def bank(name):
            return ctx.enter_context(nc.psum_tensor(name, [P, 512], F32))

        xc = sb("xc", [P, XJ, H], F32)
        arena = sb("arena", [P, 8 * CJ * H + 2 * CJ], F32)
        at = [0]

        def carve(n):
            at[0] += n
            assert at[0] <= 8 * CJ * H + 2 * CJ
            return arena[:, at[0] - n:at[0]]

        row = [carve(EC).bitcast(I32) for _ in range(2)]
        att = [carve(EC) for _ in range(2)]
        hid = [carve(EC) for _ in range(2)]
        clear = carve(CLEAR_J * S)
        mask = [carve(2 * 3 * P) for _ in range(2)]
        at[0] = 0
        agg_t = [carve(CJ * S).rearrange("p (j c) -> p j c", c=S) for _ in range(2)]
        y_t = [carve(CJ * H).rearrange("p (j c) -> p j c", c=H) for _ in range(2)]
        z_t = [carve(CJ * H).rearrange("p (j c) -> p j c", c=H) for _ in range(2)]
        sq1 = carve(CJ * H).rearrange("p (j c) -> p j c", c=H)
        sq2 = carve(CJ * H).rearrange("p (j c) -> p j c", c=H)

        col = [sb(f"col{r}", [P, 2 * C], I32) for r in range(RING)]
        zg = [sb(f"zg{r}", [P, C], I32) for r in range(RING)]
        tg = [sb(f"tg{r}", [P, C, W], F32) for r in range(RING)]
        idx = [sb(f"idx{r}", [P, C], I32) for r in range(RING)]
        zb = [sb(f"zb{q}", [P, C], BF16) for q in range(2)]
        onehot = [sb(f"onehot{q}", [P, EC], BF16) for q in range(2)]
        gated = [sb(f"gated{q}", [P, C, H], F32) for q in range(2)]
        msg = sb("msg", [P, C, H], F32)
        rhs = [sb(f"rhs{q}", [P, C, S], F32) for q in range(2)]
        agg = [sb(f"agg{q}", [P, C, S], F32) for q in range(2)]
        cnt = sb("cnt", [P, C], F32)
        moved = sb("moved", [P, C], F32)
        wj = sb("wj", [P, C], F32)
        wb = sb("wb", [P, C], F32)
        wj_a = [sb(f"wj_a{q}", [P, C], F32) for q in range(2)]
        wb_a = [sb(f"wb_a{q}", [P, C], F32) for q in range(2)]
        adapt = sb("adapt", [P, C], F32)
        picked = sb("picked", [P, C, NZ], BF16)
        msum = sb("msum", [P, C, 1], F32)
        xsum = sb("xsum", [P, 2 * CJ, 1], F32)

        srci = sb("srci", [P, NT], I32)
        srcf = sb("srcf", [P, NT], F32)
        trash = sb("trash", [P, NT], F32)
        cw = sb("cw", [P, NT], F32)
        wt = sb("wt", [P, NT], F32)
        ph = sb("ph", [P, NT], F32)
        ti = sb("ti", [P, NT], I32)
        tf = sb("tf", [P, NT], F32)

        tri = sb("tri", [P, 2 * P], F32)
        ident = sb("ident", [P, P], BF16)
        lane = sb("lane", [P, 1], F32)
        types = sb("types", [P, NZ], F32)
        w1s = sb("w1s", [R_ATTR, H], F32)
        b1s = sb("b1s", [H, 1], F32)
        w2s = sb("w2s", [H + 1, H], F32)
        embs = sb("embs", [G, NZ], F32)
        adps = sb("adps", [G, G], F32)
        vts = sb("vts", [G, NZ], F32)
        pair = [sb(f"pair{n}", [NZ, NZ], BF16) for n in range(3)]
        prest = sb("prest", [NZ, NZ], F32)
        gam = sb("gam", [P, 1, H], F32)
        bet = sb("bet", [P, 1, H], F32)
        bsum = sb("bsum", [P, 1, 1], F32)
        eps = sb("eps", [P, 1], F32)
        rt = sb("rt", [P, CJ, 1], F32)
        ss = [sb(f"ss{n}", [P, CJ, 1], F32) for n in range(2)]
        sd = [sb(f"sd{n}", [P, CJ, 1], F32) for n in range(2)]
        rs = [sb(f"rs{n}", [P, CJ, 1], F32) for n in range(2)]
        vsum = sb("vsum", [P, CJ, 1], F32)

        p_type, p_hid, p_gate, p_pair, p_agg = (bank(n) for n in ("p_type", "p_hid", "p_gate", "p_pair", "p_agg"))

        s_w = sem("s_w")
        s_x = sem("s_x")
        s_clear = sem("s_clear")
        s_zero = sem("s_zero")
        s_col = [sem(f"s_col{r}") for r in range(RING)]
        s_row = [sem(f"s_row{q}") for q in range(2)]
        s_tg = [sem(f"s_tg{r}") for r in range(RING)]
        s_zg = [sem(f"s_zg{r}") for r in range(RING)]
        s_sc = sem("s_sc")
        s_pool = sem("s_pool")
        s_pe = sem("s_pe")
        s_cst = sem("s_cst")
        s_xpad = sem("s_xpad")
        s_set = sem("s_set")
        s_vt = sem("s_vt")
        s_pair0 = sem("s_pair0")
        s_sin = sem("s_sin")
        s_zb = sem("s_zb")
        s_bc = sem("s_bc")
        s_oh = sem("s_oh")
        s_aa = sem("s_aa")
        s_ad = sem("s_ad")
        s_g1 = sem("s_g1")
        s_si = sem("s_si")
        s_g2 = sem("s_g2")
        s_wj = sem("s_wj")
        s_wb = sem("s_wb")
        s_gp = sem("s_gp")
        s_mask = sem("s_mask")
        s_moved = sem("s_moved")
        s_idx = sem("s_idx")
        s_m1 = sem("s_m1")
        s_m2 = sem("s_m2")
        s_msg = sem("s_msg")
        s_ag = sem("s_ag")
        s_ev = sem("s_ev")
        s_xs = sem("s_xs")
        s_xd = sem("s_xd")
        s_agg = [sem(f"s_agg{q}") for q in range(2)]
        s_out = [sem(f"s_out{q}") for q in range(2)]
        s_rm = sem("s_rm")
        s_rt = sem("s_rt")
        s_t = sem("s_t")
        s_z1 = sem("s_z1")
        s_y = sem("s_y")
        s_q1 = sem("s_q1")
        s_s1 = sem("s_s1")
        s_d1 = sem("s_d1")
        s_r1 = sem("s_r1")
        s_u = sem("s_u")
        s_v = sem("s_v")
        s_vs = sem("s_vs")
        s_vc = sem("s_vc")
        s_z2 = sem("s_z2")
        s_q2 = sem("s_q2")
        s_s2 = sem("s_s2")
        s_d2 = sem("s_d2")
        s_r2 = sem("s_r2")
        s_o = sem("s_o")

        SETUP_DMAS = 12
        block = ctx.enter_context(nc.Block())

        def chunks(eng, body):
            for c in range(PEEL):
                body(c, c)
            with eng.Fori(0, (NCH - PEEL) // RING) as i:
                for k in range(RING):
                    body(i * RING + (PEEL + k), PEEL + k)

        def uses(c, first, ring):
            return (c - first % ring) // ring + 1 if isinstance(c, int) else None

        def nth(c, first, ring, each):
            if isinstance(c, int):
                return (c // ring + 1) * each
            return (c - first % ring) * (each // ring) + each

        @block.sync
        def _(sp):
            def load(c, f):
                r, q = f % RING, f % 2
                if f >= RING:
                    sp.wait_ge(s_msg, c - (RING - 1))
                sp.dma_start(col[r][:, :], cols[bass.ds(c, 1)].rearrange("a p k -> (a p) k")).then_inc(s_col[r], 16)
                if f >= 2:
                    sp.wait_ge(s_mask, c - 1)
                    sp.wait_ge(s_g1, c - 1)
                sp.dma_start(row[q][:, :], src_row[bass.ds(c, 1), :].partition_broadcast(P).rearrange("p a k -> p (a k)")).then_inc(s_row[q], 16)
                sp.dma_start(att[q][0:R_ATTR, :], attr[bass.ds(c, 1)].rearrange("a r k -> (a r) k")).then_inc(s_row[q], 16)

            chunks(sp, load)

            def rows(t, k):
                return t[0:NJ * P, :].rearrange("(p j) c -> p (j c)", p=P)[:, bass.ds(k, 1)]

            for q in range(2):
                pass
            sp.wait_ge(s_sc, NCH * 2 * 32)

            def fetch(k, f):
                q = f % 2
                if f >= 2:
                    sp.wait_ge(s_t, k - 1)
                sp.dma_start(agg_t[q], sums[0:NJ * P, :].rearrange("(p j) c -> p j c", p=P)[:, bass.ds(k * CJ, CJ), :]
                             ).then_inc(s_agg[q], 16)

            def store(k, f):
                q = f % 2
                sp.wait_ge(s_o, k + 1)
                sp.dma_start(out[0:NJ * P, :].rearrange("(p j) c -> p j c", p=P)[:, bass.ds(k * CJ, CJ), :], z_t[q]
                             ).then_inc(s_out[q], 16)

            fetch(0, 0)
            fetch(1, 1)
            fetch(2, 2)
            store(0, 0)
            with sp.Fori(0, (NST - 4) // 2) as i:
                for k in range(2):
                    fetch(i * 2 + (3 + k), 3 + k)
                    store(i * 2 + (1 + k), 1 + k)
            last = NST - 1
            q = last % 2
            sp.wait_ge(s_t, last - 1)
            sp.dma_start(agg_t[q][:, 0:CJ - 1, :], sums[0:NJ * P, :].rearrange("(p j) c -> p j c", p=P)[:, last * CJ:NJ, :]).then_inc(s_agg[q], 16)
            sp.dma_start(agg_t[q][0:REST, CJ - 1, :], sums[NJ * P:N, :]).then_inc(s_agg[q], 16)
            for k in range(NST - 3, NST - 1):
                store(k, k)
            sp.wait_ge(s_o, NST)
            sp.dma_start(out[0:NJ * P, :].rearrange("(p j) c -> p j c", p=P)[:, last * CJ:NJ, :], z_t[q][:, 0:CJ - 1, :]).then_inc(s_out[q], 16)
            sp.dma_start(out[NJ * P:N, :], z_t[q][0:REST, CJ - 1, :]).then_inc(s_out[q], 16)
            sp.wait_ge(s_out[0], 16 * ((NST + 1) // 2) + (16 if q == 0 else 0))
            sp.wait_ge(s_out[1], 16 * (NST // 2) + (16 if q == 1 else 0))

        @block.gpsimd
        def _(pool):
            nc.gpsimd.memset(clear, 0.0).then_inc(s_clear, 1)
            nc.gpsimd.memset(tri[:, :], 1.0).then_inc(s_cst, 1)
            nc.gpsimd.memset(ident[:, :], 0.0).then_inc(s_cst, 1)
            nc.gpsimd.iota(lane[:, :], [[0, 1]], base=0, channel_multiplier=1,
                           allow_small_or_imprecise_dtypes=True).then_inc(s_cst, 1)
            nc.gpsimd.iota(types[:, :], [[1, NZ]], base=0, channel_multiplier=0,
                           allow_small_or_imprecise_dtypes=True).then_inc(s_cst, 1)
            nc.gpsimd.iota(trash[:, :].rearrange("p (g b) -> p g b", b=2), [[0, NT // 2], [P, 2]], base=TRASH,
                           channel_multiplier=1, allow_small_or_imprecise_dtypes=True).then_inc(s_cst, 1)
            pool.wait_ge(s_cst, 5)
            nc.gpsimd.affine_select(out=tri[:, P:2 * P], in_=tri[:, P:2 * P], compare_op=ALU.is_ge, fill=0.0,
                                    base=0, pattern=[[-1, P]], channel_multiplier=1).then_inc(s_cst, 1)
            nc.gpsimd.affine_select(out=ident[:, :], in_=ident[:, :], compare_op=ALU.not_equal, fill=1.0,
                                    base=0, pattern=[[-1, P]], channel_multiplier=1).then_inc(s_cst, 1)

            def gather(c, f, ts):
                r = f % RING
                if 0 in ts:
                    pool.wait_ge(s_col[r], nth(c, f, RING, 16))
                    if f >= RING:
                        pool.wait_ge(s_msg, c - (RING - 1))
                pool.sem_inc(s_pool, 1)
                for t in ts:
                    pool.indirect_dma_start(tg[r][:, t, :], None, table, bass.IndirectOffsetOnAxis(
                        ap=col[r][:, C + t:C + t + 1], axis=0)).then_inc(s_tg[r], 16)
                    pool.indirect_dma_start(zg[r][:, t:t + 1], None, node_z, bass.IndirectOffsetOnAxis(
                        ap=col[r][:, t:t + 1], axis=0)).then_inc(s_zg[r], 16)

            def scatter(c, f, g):
                r, q = f % RING, f % 2
                if g == 0:
                    pool.wait_ge(s_ev, c + 1)
                    pool.wait_ge(s_idx, c + 1)
                if not (f == 0 and g == 0):
                    pool.wait_ge(s_sc, c * 64 + 32 * g)
                else:
                    pool.wait_ge(s_zero, 16 * (SUM_J // (CLEAR_J * CLEAR_REP)))
                pool.sem_inc(s_pool, 1)
                for t in (2 * g, 2 * g + 1):
                    pool.indirect_dma_start(sums, bass.IndirectOffsetOnAxis(ap=idx[r][:, t:t + 1], axis=0),
                                            agg[q][:, t, :], None, compute_op=ALU.add).then_inc(s_sc, 16)

            LAG = 3

            def turn(c, f):
                gather(c, f, (0, 1))
                if f >= LAG:
                    scatter(c - LAG, f - LAG, 0)
                gather(c, f, (2, 3))
                if f >= LAG:
                    scatter(c - LAG, f - LAG, 1)

            chunks(pool, turn)
            for c in range(NCH - LAG, NCH):
                scatter(c, c, 0)
                scatter(c, c, 1)

            def mean(k, f):
                q = f % 2
                pool.wait_ge(s_rt, k + 1)
                if f >= 2:
                    pool.wait_ge(s_vc, k - 1)
                nc.gpsimd.tensor_tensor(y_t[q], agg_t[q][:, :, 0:H], rt[:, :, :].broadcast_to([P, CJ, H]), ALU.mult).then_inc(s_t, 1)
                if f >= 2:
                    pool.wait_ge(s_out[q], nth2(k, f) - 16)
                nc.gpsimd.tensor_tensor(z_t[q], xc[:, bass.ds(k * CJ, CJ), :], bet[:, :, :].broadcast_to([P, CJ, H]), ALU.add).then_inc(s_z1, 1)

            def nth2(k, f):
                if isinstance(k, int):
                    return (k // 2 + 1) * 16
                return (k - f % 2) * 8 + 16

            def first_norm(k, f):
                q = f % 2
                pool.wait_ge(s_r1, k + 1)
                nc.gpsimd.tensor_tensor(y_t[q], y_t[q], rs[0][:, :, :].broadcast_to([P, CJ, H]), ALU.mult).then_inc(s_u, 1)

            def last_norm(k, f):
                q = f % 2
                pool.wait_ge(s_r2, k + 1)
                nc.gpsimd.tensor_tensor(z_t[q], z_t[q], rs[1][:, :, :].broadcast_to([P, CJ, H]), ALU.mult).then_inc(s_o, 1)

            def step(k, f):
                mean(k, f)
                if f >= 1:
                    last_norm(k - 1, f - 1)
                first_norm(k, f)

            pool.wait_ge(s_xd, NCH - PEEL + 1)
            for k in range(4):
                step(k, k)
            with pool.Fori(0, (NST - 4) // 2) as i:
                for k in range(2):
                    step(i * 2 + (4 + k), 4 + k)
            last_norm(NST - 1, NST - 1)

        @block.scalar
        def _(act):
            act.dma_start(srci[:, :], src_col).then_inc(s_w, 16)
            act.dma_start(wt[:, :], weight).then_inc(s_w, 16)
            act.dma_start(embs[:, :], emb_t).then_inc(s_w, 16)
            act.dma_start(adps[:, :], adapt_t).then_inc(s_w, 16)
            act.dma_start(w1s[:, :], w1).then_inc(s_w, 16)
            act.dma_start(b1s[:, :], b1).then_inc(s_w, 16)
            act.dma_start(w2s[0:H, :], w2).then_inc(s_w, 16)
            act.dma_start(w2s[H:H + 1, :], b2).then_inc(s_w, 16)
            act.dma_start(gam[:, 0, :], gamma.partition_broadcast(P).rearrange("p a k -> p (a k)")).then_inc(s_w, 16)
            act.dma_start(bet[:, 0, :], beta.partition_broadcast(P).rearrange("p a k -> p (a k)")).then_inc(s_w, 16)
            act.wait_ge(s_clear, 1)
            big = CLEAR_J * CLEAR_REP
            zeros = clear.rearrange("p (a k) -> p a k", a=1).broadcast_to([P, CLEAR_REP, CLEAR_J * S])
            for n in range(SUM_J // big):
                act.dma_start(sums.rearrange("(p j) c -> p (j c)", p=P)[:, n * big * S:(n + 1) * big * S].rearrange(
                    "p (a k) -> p a k", a=CLEAR_REP), zeros).then_inc(s_zero, 16)
            act.wait_ge(s_xpad, 1)
            step = -(-NJ // X_PARTS)
            for n in range(X_PARTS):
                a, b = n * step, min(NJ, (n + 1) * step)
                act.dma_start(xc[:, a:b, :], x[0:NJ * P, :].rearrange("(p j) c -> p j c", p=P)[:, a:b, :]).then_inc(s_x, 16)
            act.dma_start(xc[0:REST, NJ, :], x[NJ * P:N, :]).then_inc(s_x, 16)

            act.wait_ge(s_set, 10)
            nc.scalar.activation(tf[:, :], ph[:, :], ACT.Sin, scale=6.283185).then_inc(s_sin, 1)
            act.wait_ge(s_w, 16 * 10)

            def chunk(c, f, tail=False):
                q = f % 2
                if not tail:
                    act.wait_ge(s_g1, c + 1)
                    if f >= 2:
                        act.wait_ge(s_g2, c - 1)
                    nc.scalar.activation(hid[q][0:H, :], p_hid[0:H, 0:EC], ACT.Silu, bias=b1s[:, :]).then_inc(s_si, 1)
                if f >= 1:
                    act.wait_ge(s_ag, c)
                    if f >= 3:
                        act.wait_ge(s_sc, (c - 2) * 64)
                    nc.scalar.activation(agg[1 - q][:, :, :].rearrange("p t k -> p (t k)"), p_agg[:, 0:C * S], ACT.Copy).then_inc(s_ev, 1)
                if not tail:
                    act.wait_ge(s_g2, c + 1)
                    act.wait_ge(s_wb, c + 1)
                    if f >= 2:
                        act.wait_ge(s_m1, c - 1)
                    for t in range(C):
                        last = nc.scalar.activation(gated[q][:, t, :], p_gate[:, t * H:(t + 1) * H], ACT.Identity,
                                                    scale=wj_a[q][:, t:t + 1], bias=wb_a[q][:, t:t + 1])
                    last.then_inc(s_gp, 1)

            chunks(act, chunk)
            chunk(NCH, NCH, tail=True)

            def step_a(k, f):
                q = f % 2
                act.wait_ge(s_y, k + 1)
                if f >= 1:
                    act.wait_ge(s_s1, k)
                nc.scalar.activation(sq1, y_t[q], ACT.Square).then_inc(s_q1, 1)

            def step_b(k, f):
                q = f % 2
                act.wait_ge(s_z2, k + 1)
                if f >= 1:
                    act.wait_ge(s_s2, k)
                nc.scalar.activation(sq2, z_t[q], ACT.Square).then_inc(s_q2, 1)

            def root_a(k, f):
                act.wait_ge(s_s1, k + 1)
                if f >= 1:
                    act.wait_ge(s_r1, k)
                nc.scalar.activation(sd[0][:, :, :], ss[0][:, :, :], ACT.Sqrt, scale=1.0 / H, bias=eps[:, :]).then_inc(s_d1, 1)

            def root_b(k, f):
                act.wait_ge(s_s2, k + 1)
                if f >= 1:
                    act.wait_ge(s_r2, k)
                nc.scalar.activation(sd[1][:, :, :], ss[1][:, :, :], ACT.Sqrt, scale=1.0 / H, bias=eps[:, :]).then_inc(s_d2, 1)

            def step(k, f):
                if f >= 1:
                    step_b(k - 1, f - 1)
                step_a(k, f)
                if f >= 1:
                    root_b(k - 1, f - 1)
                root_a(k, f)

            for k in range(4):
                step(k, k)
            with act.Fori(0, (NST - 4) // 2) as i:
                for k in range(2):
                    step(i * 2 + (4 + k), 4 + k)
            step_b(NST - 1, NST - 1)
            root_b(NST - 1, NST - 1)

        @block.vector
        def _(dve):
            done = [0]

            def link(ins):
                done[0] += 1
                ins.then_inc(s_set, 1)
                dve.wait_ge(s_set, done[0])

            V = nc.vector
            V.memset(xc[:, NJ, :], 0.0).then_inc(s_xpad, 1)
            V.memset(eps[:, :], EPS)
            for q in range(2):
                link(V.memset(hid[q][0:H + 1, :], 1.0))
            dve.wait_ge(s_w, 16 * 10)
            link(V.tensor_scalar(ph[:, :], wt[:, :], 1.0 / (2 * CUTOFF), None, ALU.mult))
            link(V.tensor_copy(ti[:, :], ph[:, :]))
            link(V.tensor_copy(tf[:, :], ti[:, :]))
            link(V.scalar_tensor_tensor(ph[:, :], ph[:, :], 0.25, tf[:, :], ALU.add, ALU.subtract))
            link(V.tensor_scalar(tf[:, :], ph[:, :], 0.5, None, ALU.is_gt))
            link(V.tensor_tensor(ph[:, :], ph[:, :], tf[:, :], ALU.subtract))
            link(V.tensor_scalar(tf[:, :], ph[:, :], -0.5, None, ALU.is_lt))
            link(V.tensor_tensor(ph[:, :], ph[:, :], tf[:, :], ALU.add))
            assert done[0] == 10
            link(V.tensor_copy(srcf[:, :], srci[:, :]))
            dve.wait_ge(s_cst, 7)
            link(V.tensor_tensor(trash[:, :], trash[:, :], srcf[:, :], ALU.subtract))
            link(V.reduce_sum(bsum[:, :, :], bet[:, :, :], axis=AX_X))
            link(V.scalar_tensor_tensor(bet[:, :, :], bsum[:, :, :].broadcast_to([P, 1, H]), -1.0 / H, bet[:, :, :], ALU.mult, ALU.add))
            dve.wait_ge(s_sin, 1)
            link(V.tensor_scalar(tf[:, :], tf[:, :], 0.5, 0.5, ALU.mult, ALU.add))
            link(V.scalar_tensor_tensor(cw[:, :], wt[:, :], CUTOFF, tf[:, :], ALU.is_lt, ALU.mult))
            dve.wait_ge(s_vt, 1)
            link(V.tensor_copy(vts[:, :], p_hid[0:G, 0:NZ]))
            s_vts = done[0]
            dve.wait_ge(s_pair0, 1)
            link(V.tensor_copy(prest[:, :], p_pair[0:NZ, 0:NZ]))
            for n in range(3):
                link(V.tensor_copy(pair[n][:, :], prest[:, :]))
                if n < 2:
                    link(V.tensor_tensor(prest[:, :], prest[:, :], pair[n][:, :], ALU.subtract))
            assert done[0] == SET_TOTAL and s_vts == SET_VTS

            def chunk(c, f, tail=False):
                r, q = f % RING, f % 2
                if not tail:
                    dve.wait_ge(s_zg[r], nth(c, f, RING, 64))
                    V.tensor_copy(zb[q][:, :], zg[r][:, :]).then_inc(s_zb, 1)
                    dve.wait_ge(s_row[q], nth(c, f, 2, 32))
                    if f >= 2:
                        dve.wait_ge(s_ag, c - 1)
                    if f >= 1:
                        dve.wait_ge(s_moved, c)
                    for g in range(2):
                        for b in range(2):
                            t = 2 * g + b
                            last = V.scalar_tensor_tensor(
                                mask[q][:, g * 3 * P + b * P:g * 3 * P + b * P + (b + 1) * P],
                                row[q][:, 2 * g * P:(2 * g + b + 1) * P], srcf[:, bass.ds(c * C + t, 1)],
                                tri[:, (1 - b) * P:2 * P], ALU.is_equal, ALU.mult, accum_out=cnt[:, t:t + 1])
                    last.then_inc(s_mask, 1)
                    if f >= PEEL:
                        lo = (c - PEEL) * CJ
                        if f == PEEL:
                            dve.wait_ge(s_x, 16 * (X_PARTS + 1))
                        V.reduce_sum(xsum[:, 0:CJ, :], xc[:, bass.ds(lo, CJ), :], axis=AX_X).then_inc(s_xs, 1)
                    dve.wait_ge(s_bc, c + 1)
                    if f >= 2:
                        dve.wait_ge(s_aa, c - 1)
                    V.tensor_scalar(onehot[q][:, :], p_type[:, 0:EC], lane[:, :], None, ALU.is_equal).then_inc(s_oh, 1)
                    dve.wait_ge(s_mask, c + 1)
                    V.scalar_tensor_tensor(moved[:, :], cnt[:, :], 1.5, trash[:, bass.ds(c * C, C)],
                                           ALU.is_gt, ALU.mult).then_inc(s_moved, 1)
                if f >= 1:
                    pr = (f - 1) % RING
                    dve.wait_ge(s_gp, c)
                    V.tensor_tensor(msg[:, :, :], gated[1 - q][:, :, :], tg[pr][:, :, 0:H], ALU.mult).then_inc(s_m1, 1)
                if not tail:
                    if f >= PEEL:
                        dve.wait_ge(s_xs, c - (PEEL - 1))
                        V.scalar_tensor_tensor(xc[:, bass.ds(lo, CJ), :], xsum[:, 0:CJ, :].broadcast_to([P, CJ, H]), -1.0 / H,
                                               xc[:, bass.ds(lo, CJ), :], ALU.mult, ALU.add).then_inc(s_xd, 1)
                    dve.wait_ge(s_moved, c + 1)
                    if f >= RING:
                        dve.wait_ge(s_sc, (c - (RING - 1)) * 64)
                    V.tensor_tensor(idx[r][:, :], moved[:, :], srcf[:, bass.ds(c * C, C)], ALU.add).then_inc(s_idx, 1)
                if f >= 1:
                    dve.wait_ge(s_m1, c)
                    V.reduce_sum(msum[:, :, :], msg[:, :, :], axis=AX_X).then_inc(s_m2, 1)
                if not tail:
                    dve.wait_ge(s_tg[r], nth(c, f, RING, 64))
                    if f >= 2:
                        dve.wait_ge(s_gp, c - 1)
                    V.tensor_tensor(wj_a[q][:, :], cw[:, bass.ds(c * C, C)], tg[r][:, :, H], ALU.mult).then_inc(s_wj, 1)
                if f >= 1:
                    if f >= 3:
                        dve.wait_ge(s_ag, c - 2)
                    V.tensor_copy(rhs[1 - q][:, :, H], tg[pr][:, :, H])
                    dve.wait_ge(s_m2, c)
                    V.scalar_tensor_tensor(rhs[1 - q][:, :, 0:H], msum[:, :, :].broadcast_to([P, C, H]), -1.0 / H,
                                           msg[:, :, :], ALU.mult, ALU.add).then_inc(s_msg, 1)
                if not tail:
                    dve.wait_ge(s_aa, c + 1)
                    for t in range(C):
                        last = V.scalar_tensor_tensor(picked[:, t, :], types[:, :], tg[r][:, t, H + 1:H + 2].bitcast(I32),
                                                      p_pair[:, t * NZ:(t + 1) * NZ], ALU.is_equal, ALU.mult,
                                                      accum_out=adapt[:, t:t + 1])
                    last.then_inc(s_ad, 1)
                    dve.wait_ge(s_ad, c + 1)
                    V.tensor_tensor(wb_a[q][:, :], wj_a[q][:, :], adapt[:, :], ALU.mult).then_inc(s_wb, 1)

            chunks(dve, chunk)
            chunk(NCH, NCH, tail=True)
            lo = (NCH - PEEL) * CJ
            V.reduce_sum(xsum[:, :, :], xc[:, lo:XJ, :], axis=AX_X).then_inc(s_xs, 1)
            dve.wait_ge(s_xs, NCH - PEEL + 1)
            V.scalar_tensor_tensor(xc[:, lo:XJ, :], xsum[:, :, :].broadcast_to([P, XJ - lo, H]), -1.0 / H,
                                   xc[:, lo:XJ, :], ALU.mult, ALU.add).then_inc(s_xd, 1)

            def scale(k, f):
                q = f % 2
                if isinstance(k, int):
                    dve.wait_ge(s_agg[q], (k // 2 + 1) * 16 + (16 if k == NST - 1 else 0))
                else:
                    dve.wait_ge(s_agg[q], (k - f % 2) * 8 + 16)
                if f >= 1:
                    dve.wait_ge(s_t, k)
                V.tensor_scalar(rt[:, :, :], agg_t[q][:, :, H:S], TOT_MIN, None, ALU.max).then_inc(s_rm, 1)
                dve.wait_ge(s_rm, k + 1)
                V.reciprocal(rt[:, :, :], rt[:, :, :]).then_inc(s_rt, 1)

            def residual(k, f):
                q = f % 2
                dve.wait_ge(s_u, k + 1)
                V.tensor_tensor(y_t[q], y_t[q], gam[:, :, :].broadcast_to([P, CJ, H]), ALU.mult).then_inc(s_v, 1)
                dve.wait_ge(s_v, k + 1)
                V.reduce_sum(vsum[:, :, :], y_t[q], axis=AX_X).then_inc(s_vs, 1)
                dve.wait_ge(s_z1, k + 1)
                V.tensor_tensor(z_t[q], z_t[q], y_t[q], ALU.add).then_inc(s_vc, 1)
                dve.wait_ge(s_vs, k + 1)
                dve.wait_ge(s_vc, k + 1)
                V.scalar_tensor_tensor(z_t[q], vsum[:, :, :].broadcast_to([P, CJ, H]), -1.0 / H, z_t[q],
                                       ALU.mult, ALU.add).then_inc(s_z2, 1)

            def sum_b(k, f):
                dve.wait_ge(s_q2, k + 1)
                V.reduce_sum(ss[1][:, :, :], sq2, axis=AX_X).then_inc(s_s2, 1)

            def step(k, f):
                q = f % 2
                scale(k, f)
                if f >= 1:
                    residual(k - 1, f - 1)
                dve.wait_ge(s_t, k + 1)
                V.tensor_tensor(y_t[q], y_t[q], xc[:, bass.ds(k * CJ, CJ), :], ALU.add).then_inc(s_y, 1)
                if f >= 1:
                    sum_b(k - 1, f - 1)
                dve.wait_ge(s_q1, k + 1)
                V.reduce_sum(ss[0][:, :, :], sq1, axis=AX_X).then_inc(s_s1, 1)
                if f >= 1:
                    dve.wait_ge(s_d2, k)
                    if f >= 2:
                        dve.wait_ge(s_o, k - 1)
                    V.reciprocal(rs[1][:, :, :], sd[1][:, :, :]).then_inc(s_r2, 1)
                dve.wait_ge(s_d1, k + 1)
                if f >= 1:
                    dve.wait_ge(s_u, k)
                V.reciprocal(rs[0][:, :, :], sd[0][:, :, :]).then_inc(s_r1, 1)

            for k in range(4):
                step(k, k)
            with dve.Fori(0, (NST - 4) // 2 - 1) as i:
                for k in range(2):
                    step(i * 2 + (4 + k), 4 + k)
            for k in range(NST - 2, NST):
                step(k, k)
            k = NST - 1
            residual(k, k)
            sum_b(k, k)
            dve.wait_ge(s_d2, k + 1)
            dve.wait_ge(s_o, k)
            V.reciprocal(rs[1][:, :, :], sd[1][:, :, :]).then_inc(s_r2, 1)

        @block.tensor
        def _(pe):
            mm = nc.tensor.matmul
            pe.wait_ge(s_w, 16 * 10)
            mm(p_hid[0:G, 0:NZ], adps[:, :], embs[:, :], start=True, stop=True).then_inc(s_vt, 1)
            pe.wait_ge(s_set, SET_VTS)
            mm(p_pair[0:NZ, 0:NZ], embs[:, :], vts[:, :], start=True, stop=True).then_inc(s_pair0, 1)
            pe.wait_ge(s_set, SET_TOTAL)
            pe.wait_ge(s_cst, 7)

            def chunk(c, f, tail=False):
                q = f % 2
                if not tail:
                    pe.wait_ge(s_row[q], nth(c, f, 2, 32))
                    if f >= 1:
                        pe.wait_ge(s_si, c)
                    pe.sem_inc(s_pe, 1)
                    mm(p_hid[0:H, 0:EC], w1s[:, :], att[q][0:R_ATTR, :], start=True, stop=True).then_inc(s_g1, 1)
                    pe.wait_ge(s_zb, c + 1)
                    if f >= 1:
                        pe.wait_ge(s_oh, c)
                    for t in range(C):
                        last = mm(p_type[:, t * P:(t + 1) * P], zb[q][:, t:t + 1].broadcast_to([P, P]), ident[:, :],
                                  start=True, stop=True)
                    last.then_inc(s_bc, 1)
                    pe.wait_ge(s_oh, c + 1)
                    if f >= 1:
                        pe.wait_ge(s_ad, c)
                    for t in range(C):
                        for n in range(3):
                            last = mm(p_pair[:, t * NZ:(t + 1) * NZ], onehot[q][0:NZ, t * P:(t + 1) * P], pair[n][:, :],
                                      start=(n == 0), stop=(n == 2))
                    last.then_inc(s_aa, 1)
                    pe.wait_ge(s_si, c + 1)
                    if f >= 1:
                        pe.wait_ge(s_gp, c)
                    for t in range(C):
                        last = mm(p_gate[:, t * H:(t + 1) * H], hid[q][0:H + 1, t * P:(t + 1) * P], w2s[:, :],
                                  start=True, stop=True)
                    last.then_inc(s_g2, 1)
                if f >= 1:
                    pe.wait_ge(s_msg, c)
                    if f >= 2:
                        pe.wait_ge(s_ev, c - 1)
                    m, v = mask[1 - q], rhs[1 - q]
                    for g in range(2):
                        o = g * 3 * P
                        t = 2 * g
                        mm(p_agg[:, t * S:(t + 1) * S], m[:, o:o + P], v[:, t, :], start=True, stop=False)
                        mm(p_agg[:, t * S:(t + 1) * S], m[:, o + P:o + 2 * P], v[:, t + 1, :], start=False, stop=True)
                        last = mm(p_agg[:, (t + 1) * S:(t + 2) * S], m[:, o + 2 * P:o + 3 * P], v[:, t + 1, :],
                                  start=True, stop=True)
                    last.then_inc(s_ag, 1)

            chunks(pe, chunk)
            chunk(NCH, NCH, tail=True)


SET_VTS = 17
SET_TOTAL = 23


def kernel(x, src, dst, edge_attr_40, edge_weight, node_type_119, node_vec, L0_gnn_W1, L0_gnn_b1, L0_gnn_W2, L0_gnn_b2,
           L0_gnn_emb, L0_gnn_adaptW, L0_gnn_gamma, L0_gnn_beta):
    import numpy as np
    import concourse.bacc as bacc
    from concourse.bass_utils import run_bass_kernel_spmd

    def padded(a, fill):
        rows = np.full((EPAD - E,) + a.shape[1:], fill, a.dtype)
        return np.concatenate([np.asarray(a), rows])

    x = np.asarray(x)
    table = np.empty((N, W), np.float32)
    table[:, 0:H] = x
    table[:, H] = np.asarray(node_vec)
    table.view(np.int32)[:, H + 1] = np.asarray(node_type_119)
    src_p = padded(src, PAD_ROW)
    src_g = padded(src, 0)
    dst_p = padded(dst, 0)
    cols = np.concatenate([a.reshape(NCH, C, P).transpose(0, 2, 1) for a in (src_g, dst_p)], axis=2)
    arrays = {
        "in_x": x,
        "in_table": table,
        "in_src_row": src_p.reshape(NCH, EC),
        "in_cols": cols,
        "in_src_col": src_p.reshape(NT, P).T,
        "in_weight": padded(edge_weight, 0).reshape(NT, P).T,
        "in_attr": padded(edge_attr_40, 0).reshape(NCH, EC, R_ATTR).transpose(0, 2, 1),
        "in_node_z": np.asarray(node_type_119).reshape(N, 1),
        "in_w1": np.asarray(L0_gnn_W1).T,
        "in_b1": np.asarray(L0_gnn_b1).reshape(H, 1),
        "in_w2": np.asarray(L0_gnn_W2).T,
        "in_b2": np.asarray(L0_gnn_b2).reshape(1, H),
        "in_emb_t": np.asarray(L0_gnn_emb).T,
        "in_adapt_t": np.asarray(L0_gnn_adaptW).T,
        "in_gamma": np.asarray(L0_gnn_gamma).reshape(1, H),
        "in_beta": np.asarray(L0_gnn_beta).reshape(1, H),
    }
    arrays = {k: np.ascontiguousarray(a) for k, a in arrays.items()}
    nc = bacc.Bacc("TRN2", target_bir_lowering=False, num_devices=1)
    args = [nc.dram_tensor(k, a.shape, mybir.dt.from_np(a.dtype), kind="ExternalInput").ap() for k, a in arrays.items()]
    out = nc.dram_tensor("out", (N, H), F32, kind="ExternalOutput").ap()
    gnn_resnorm(nc, *args, out)
    r = run_bass_kernel_spmd(nc, [arrays], core_ids=[0])
    return r.results[0]["out"]
```

```python
from contextlib import ExitStack

import concourse.bass as bass
from concourse import mybir

ALU = mybir.AluOpType
ACT = mybir.ActivationFunctionType
BF16 = mybir.dt.bfloat16
F32 = mybir.dt.float32
I32 = mybir.dt.int32
AX_X = mybir.AxisListType.X

P = 128
N = 100000
H = 48
E = 25000
R_ATTR = 40
NZ = 119
G = 32
CUTOFF = 6.0
EPS = 1e-5
TOT_MIN = 1e-8

C = 4
EC = C * P
NCH = -(-E // EC)
EPAD = NCH * EC
NT = NCH * C
RING = 4
PEEL = RING + 1
assert (NCH - PEEL) % RING == 0

W = H + 2
S = H + 1
TRASH = N
PAD_ROW = N + 2 * P
SUM_J = 784
SUM_ROWS = P * SUM_J
CLEAR_J = 28
CLEAR_REP = 4
assert SUM_ROWS > PAD_ROW and SUM_J % (CLEAR_J * CLEAR_REP) == 0

ZK = 4
ZR = ZK * P
ZW = -(-N // ZR)

NJ = N // P
REST = N - NJ * P
XJ = NJ + 1
CJ = 17
CA = 10
TRING = 4
NST = XJ // CJ
TPEEL = 6
assert (NST - TPEEL) % TRING == 0
ARENA = 14900
BK = 65
assert NST * CJ == XJ
XLOOP = (NCH - PEEL) * CJ


SET_PHASE = 11
SET_VTS = 40
SET_TOTAL = 46
TRAIL = 7
OA, OB, OC = 4, 11, 14
LAST = 5


def gnn_resnorm(nc, x, table, src_row, cols, src_col, weight, attr, z_rows, z_before, w1, b1, w2, b2, emb_t, adapt_t,
                gamma, beta, out):
    sums = nc.dram_tensor("sums", (SUM_ROWS, S), F32, kind="Internal").ap()
    ctx = ExitStack()
    with ctx:
        def sb(name, shape, dt):
            return ctx.enter_context(nc.sbuf_tensor(name, shape, dt))

        def sem(name):
            return ctx.enter_context(nc.semaphore(name))

        def bank(name):
            return ctx.enter_context(nc.psum_tensor(name, [P, 512], F32))

        xc = sb("xc", [P, XJ, H], F32)
        arena = sb("arena", [P, ARENA], F32)
        at = [0]

        def carve(n, dt=F32, parts=P):
            size = n if dt != BF16 else -(-n // 2)
            at[0] += size
            assert at[0] <= ARENA
            a = arena[0:parts, at[0] - size:at[0]]
            return (a if dt == F32 else a.bitcast(dt))[:, 0:n]

        def carve3(j, k, dt=F32, parts=P):
            return carve(j * k, dt, parts).rearrange("p (j k) -> p j k", k=k)

        row = [carve(EC, I32) for _ in range(2)]
        att = [carve(EC) for _ in range(2)]
        hid = [carve(EC) for _ in range(2)]
        clear = carve(CLEAR_J * S)
        over = at[0]
        mask = [carve(2 * 3 * P) for _ in range(2)]
        end = at[0]
        at[0] = over
        wt, ph, tf = carve(NT), carve(NT), carve(NT)
        ti = carve(NT, I32)
        assert at[0] <= end
        at[0] = end
        over = at[0]
        above = [carve3(ZK, EC, BF16) for _ in range(2)]
        end = at[0]
        at[0] = over
        z_own, z_bef = carve3(ZK, ZW, I32), carve3(ZK, ZW, I32)
        assert at[0] <= end
        at[0] = end
        col = [carve(C, I32) for _ in range(RING)]
        tg = [carve3(C, W) for _ in range(RING)]
        idx = [carve(C, I32) for _ in range(RING)]
        zb = [carve(C, BF16) for _ in range(2)]
        apart = [carve(EC, BF16) for _ in range(2)]
        onehot = [carve(EC, BF16) for _ in range(2)]
        gated = [carve3(C, H) for _ in range(2)]
        msg = carve3(C, H)
        rhs = [carve3(C, S) for _ in range(2)]
        agg = [carve3(C, S) for _ in range(2)]
        wj_a = [carve(C) for _ in range(2)]
        wb_a = [carve(C) for _ in range(2)]
        cnt, moved, adapt, z2 = carve(C), carve(C), carve(C), carve(C)
        picked = carve3(C, NZ, BF16)
        found = carve3(C, ZW, BF16)
        msum = carve3(C, 1)
        xsum = carve3(2 * CJ, 1)
        srci = carve(NT, I32)
        srcf, trash, cw, zcol = carve(NT), carve(NT), carve(NT), carve(NT)
        zdiff = carve3(ZK, ZW, BF16)
        tri = carve(2 * P)
        ident = carve(P, BF16)
        lane = carve(1)
        flip = carve(ZK)
        edge = carve(ZK)
        types = carve(NZ)
        nodes = carve(ZW)
        w1s = carve(H, parts=R_ATTR)
        b1s = carve(1, parts=H)
        w2s = carve(H, parts=H + 1)
        embs, vts = carve(NZ, parts=G), carve(NZ, parts=G)
        adps = carve(G, parts=G)
        pair = [carve(NZ, BF16, parts=NZ) for _ in range(3)]
        prest = carve(NZ, parts=NZ)
        edge_end = at[0]

        at[0] = 0
        agg_t = [carve3(CJ, S) for _ in range(TRING)]
        y_t = [carve3(CJ, H) for _ in range(TRING)]
        z_t = [carve3(CJ, H) for _ in range(TRING)]
        sq1 = carve3(CJ, H)
        sq2 = carve3(CJ, H)

        gam = sb("gam", [P, 1, H], F32)
        bet = sb("bet", [P, 1, H], F32)
        bsum = sb("bsum", [P, 1, 1], F32)
        eps = sb("eps", [P, 1], F32)
        identf = sb("identf", [P, P], F32)
        ones = sb("ones", [BK, P], BF16)
        bet_k = sb("bet_k", [BK, 1, H], BF16)
        rm = sb("rm", [P, CJ, 1], F32)
        rt = [sb(f"rt{n}", [P, CJ, 1], F32) for n in range(2)]
        ss = [sb(f"ss{n}", [P, CJ, 1], F32) for n in range(2)]
        sd = [sb(f"sd{n}", [P, CJ, 1], F32) for n in range(2)]
        rs1 = [sb(f"rs1_{n}", [P, CJ, 1], F32) for n in range(2)]
        rs2 = [sb(f"rs2_{n}", [P, CJ, 1], F32) for n in range(2)]
        bet_part = sb("bet_part", [P, 1, H], BF16)
        vsum = [sb(f"vsum{n}", [P, CJ, 1], F32) for n in range(2)]

        ps = [ctx.enter_context(nc.psum_tensor(f"ps{n}", [P, 2, 512], F32)) for n in range(4)]
        p_type, p_hid = ps[0][:, 0, :], ps[0][:, 1, :]
        p_gate, p_pair = ps[1][:, 0, :], ps[1][:, 1, :]
        p_agg = ps[2][:, 0, :]
        p_look = [ps[3][:, n, :] for n in range(2)]
        p_z = ps[0:2]

        s_w = sem("s_w")
        s_x = sem("s_x")
        s_xp = [sem(f"s_xp{r}") for r in range(RING)]
        s_clear = sem("s_clear")
        s_zero = sem("s_zero")
        s_col = [sem(f"s_col{r}") for r in range(RING)]
        s_row = [sem(f"s_row{q}") for q in range(2)]
        s_tg = [sem(f"s_tg{r}") for r in range(RING)]
        s_sc = sem("s_sc")
        s_pool = sem("s_pool")
        s_pe = sem("s_pe")
        s_cst = sem("s_cst")
        s_xpad = sem("s_xpad")
        s_set = sem("s_set")
        s_vt = sem("s_vt")
        s_pair0 = sem("s_pair0")
        s_sin = sem("s_sin")
        s_ab = sem("s_ab")
        s_apart = sem("s_apart")
        s_look = sem("s_look")
        s_found = sem("s_found")
        s_zb = sem("s_zb")
        s_bc = sem("s_bc")
        s_oh = sem("s_oh")
        s_aa = sem("s_aa")
        s_ad = sem("s_ad")
        s_g1 = sem("s_g1")
        s_si = sem("s_si")
        s_g2 = sem("s_g2")
        s_wj = sem("s_wj")
        s_wb = sem("s_wb")
        s_gp = sem("s_gp")
        s_mask = sem("s_mask")
        s_moved = sem("s_moved")
        s_idx = sem("s_idx")
        s_m1 = sem("s_m1")
        s_m2 = sem("s_m2")
        s_msg = sem("s_msg")
        s_ag = sem("s_ag")
        s_ev = sem("s_ev")
        s_xs = sem("s_xs")
        s_xd = sem("s_xd")
        s_agg = [sem(f"s_agg{q}") for q in range(TRING)]
        s_out = [sem(f"s_out{q}") for q in range(TRING)]
        s_rm, s_rt, s_t, s_y, s_q1, s_s1, s_d1, s_r1, s_u, s_v, s_vs, s_pz, s_z, s_q2, s_s2, s_d2, s_r2, s_o, s_op = (
            sem(n) for n in ("s_rm", "s_rt", "s_t", "s_y", "s_q1", "s_s1", "s_d1", "s_r1", "s_u", "s_v", "s_vs",
                             "s_pz", "s_z", "s_q2", "s_s2", "s_d2", "s_r2", "s_o", "s_op"))

        block = ctx.enter_context(nc.Block())

        def chunks(eng, body):
            for c in range(PEEL):
                body(c, c)
            with eng.Fori(0, (NCH - PEEL) // RING) as i:
                for k in range(RING):
                    body(i * RING + (PEEL + k), PEEL + k)

        def nth(c, first, ring, each):
            if isinstance(c, int):
                return (c // ring + 1) * each
            return (c - first % ring) * (each // ring) + each

        def turns(eng, body):
            for n in range(TPEEL):
                body(n, n, lambda lag, n=n: n >= lag)
            with eng.Fori(0, (NST - TPEEL) // TRING) as i:
                for k in range(TRING):
                    body(i * TRING + (TPEEL + k), TPEEL + k, lambda lag: True)
            for n in range(NST, NST + LAST):
                body(n, n, lambda lag, n=n: n - lag < NST)

        @block.sync
        def _(sp):
            x_v = x[0:NJ * P, :].rearrange("(p j) c -> p j c", p=P)
            for r in range(TRING):
                sp.sem_inc(s_out[r], 16)

            def load(c, f):
                r, q = f % RING, f % 2
                if f >= RING:
                    sp.wait_ge(s_msg, c - (RING - 1))
                if f == PEEL - 1:
                    sp.wait_ge(s_xpad, 1)
                    sp.dma_start(xc[:, XLOOP:NJ, :], x_v[:, XLOOP:NJ, :]).then_inc(s_x, 16)
                    sp.dma_start(xc[0:REST, NJ, :], x[NJ * P:N, :]).then_inc(s_x, 16)
                if f >= PEEL:
                    lo = (c - PEEL) * CJ
                    sp.dma_start(xc[:, bass.ds(lo, CJ), :], x_v[:, bass.ds(lo, CJ), :]).then_inc(s_xp[f % RING], 16)
                sp.dma_start(col[r][:, :], cols[bass.ds(c, 1)].rearrange("a p k -> (a p) k")).then_inc(s_col[r], 16)
                if f >= 2:
                    sp.wait_ge(s_mask, c - 1)
                    sp.wait_ge(s_g1, c - 1)
                    sp.wait_ge(s_ab, c - 1)
                sp.dma_start(row[q][:, :], src_row[bass.ds(c, 1), :].partition_broadcast(P).rearrange("p a k -> p (a k)")).then_inc(s_row[q], 16)
                sp.dma_start(att[q][0:R_ATTR, :], attr[bass.ds(c, 1)].rearrange("a r k -> (a r) k")).then_inc(s_row[q], 16)

            chunks(sp, load)

            sums_v = sums[0:NJ * P, :].rearrange("(p j) c -> p j c", p=P)
            out_v = out[0:NJ * P, :].rearrange("(p j) c -> p j c", p=P)
            sp.wait_ge(s_sc, NCH * 64)
            sp.wait_ge(s_gp, NCH)
            sp.wait_ge(s_ag, NCH)

            def fetch(k, f):
                q = f % TRING
                if f >= TRING:
                    sp.wait_ge(s_t, k - (TRING - 1))
                for a, b in ((0, CJ // 2), (CJ // 2, CJ)):
                    sp.dma_start(agg_t[q][:, a:b, :], sums_v[:, bass.ds(k * CJ + a, b - a), :]).then_inc(s_agg[q], 16)

            def store(k, f):
                sp.wait_ge(s_o, k + 1)
                sp.wait_ge(s_op, k + 1)
                sp.dma_start(out_v[:, bass.ds(k * CJ, CJ), :], z_t[f % TRING]).then_inc(s_out[f % TRING], 16)

            first = TRAIL + 2
            for k in range(first):
                fetch(k, k)
                if k >= TRAIL:
                    store(k - TRAIL, k - TRAIL)
            last = NST - 1
            assert (last - first) % TRING == 0
            with sp.Fori(0, (last - first) // TRING) as i:
                for k in range(TRING):
                    fetch(i * TRING + (first + k), first + k)
                    store(i * TRING + (first + k - TRAIL), first + k - TRAIL)
            q = last % TRING
            sp.wait_ge(s_t, last - (TRING - 1))
            sp.dma_start(agg_t[q][:, 0:CJ - 1, :], sums_v[:, last * CJ:NJ, :]).then_inc(s_agg[q], 16)
            sp.dma_start(agg_t[q][0:REST, CJ - 1, :], sums[NJ * P:N, :]).then_inc(s_agg[q], 16)
            for k in range(last - TRAIL, last):
                store(k, k)
            sp.wait_ge(s_o, NST)
            sp.wait_ge(s_op, NST)
            sp.dma_start(out_v[:, last * CJ:NJ, :], z_t[q][:, 0:CJ - 1, :]).then_inc(s_out[q], 16)
            sp.dma_start(out[NJ * P:N, :], z_t[q][0:REST, CJ - 1, :]).then_inc(s_out[q], 16)
            for r in range(TRING):
                sp.wait_ge(s_out[r], 16 * (1 + len(range(r, NST, TRING)) + (r == q)))

        @block.gpsimd
        def _(pool):
            nc.gpsimd.memset(clear, 0.0).then_inc(s_clear, 1)
            nc.gpsimd.memset(tri[:, :], 1.0).then_inc(s_cst, 1)
            nc.gpsimd.memset(ident[:, :], 0.0).then_inc(s_cst, 1)
            nc.gpsimd.iota(lane[:, :], [[0, 1]], base=0, channel_multiplier=-1,
                           allow_small_or_imprecise_dtypes=True).then_inc(s_cst, 1)
            nc.gpsimd.iota(types[:, :], [[1, NZ]], base=0, channel_multiplier=0,
                           allow_small_or_imprecise_dtypes=True).then_inc(s_cst, 1)
            nc.gpsimd.iota(trash[:, :].rearrange("p (g b) -> p g b", b=2), [[0, NT // 2], [P, 2]], base=TRASH,
                           channel_multiplier=1, allow_small_or_imprecise_dtypes=True).then_inc(s_cst, 1)
            nc.gpsimd.iota(nodes[:, :], [[1, ZW]], base=0, channel_multiplier=0,
                           allow_small_or_imprecise_dtypes=True).then_inc(s_cst, 1)
            nc.gpsimd.iota(edge[:, :], [[-P * ZW, ZK]], base=0, channel_multiplier=-ZW,
                           allow_small_or_imprecise_dtypes=True).then_inc(s_cst, 1)
            nc.gpsimd.memset(flip[:, :], -1.0).then_inc(s_cst, 1)
            nc.gpsimd.memset(identf[:, :], 0.0).then_inc(s_cst, 1)
            nc.gpsimd.memset(ones[:, :], 1.0).then_inc(s_cst, 1)
            pool.wait_ge(s_cst, 10)
            nc.gpsimd.affine_select(out=identf[:, :], in_=identf[:, :], compare_op=ALU.not_equal, fill=1.0,
                                    base=0, pattern=[[-1, P]], channel_multiplier=1).then_inc(s_cst, 1)
            nc.gpsimd.affine_select(out=flip[:, :], in_=flip[:, :], compare_op=ALU.not_equal, fill=1.0,
                                    base=0, pattern=[[P, ZK]], channel_multiplier=1).then_inc(s_cst, 1)
            nc.gpsimd.affine_select(out=tri[:, P:2 * P], in_=tri[:, P:2 * P], compare_op=ALU.is_ge, fill=0.0,
                                    base=0, pattern=[[-1, P]], channel_multiplier=1).then_inc(s_cst, 1)
            nc.gpsimd.affine_select(out=ident[:, :], in_=ident[:, :], compare_op=ALU.not_equal, fill=1.0,
                                    base=0, pattern=[[-1, P]], channel_multiplier=1).then_inc(s_cst, 1)

            def gather(c, f, ts):
                r = f % RING
                if 0 in ts:
                    pool.wait_ge(s_col[r], nth(c, f, RING, 16))
                    if f >= RING:
                        pool.wait_ge(s_msg, c - (RING - 1))
                pool.sem_inc(s_pool, 1)
                for t in ts:
                    pool.indirect_dma_start(tg[r][:, t, :], None, table, bass.IndirectOffsetOnAxis(
                        ap=col[r][:, t:t + 1], axis=0)).then_inc(s_tg[r], 16)

            def scatter(c, f, g):
                r, q = f % RING, f % 2
                if g == 0:
                    pool.wait_ge(s_ev, c + 1)
                    pool.wait_ge(s_idx, c + 1)
                if not (f == 0 and g == 0):
                    pool.wait_ge(s_sc, c * 64 + 32 * g)
                else:
                    pool.wait_ge(s_zero, 16 * (SUM_J // (CLEAR_J * CLEAR_REP)))
                pool.sem_inc(s_pool, 1)
                for t in (2 * g, 2 * g + 1):
                    pool.indirect_dma_start(sums, bass.IndirectOffsetOnAxis(ap=idx[r][:, t:t + 1], axis=0),
                                            agg[q][:, t, :], None, compute_op=ALU.add).then_inc(s_sc, 16)

            LAG = 3

            def turn(c, f):
                gather(c, f, (0, 1))
                if f >= LAG:
                    scatter(c - LAG, f - LAG, 0)
                gather(c, f, (2, 3))
                if f >= LAG:
                    scatter(c - LAG, f - LAG, 1)

            chunks(pool, turn)
            for c in range(NCH - LAG, NCH):
                scatter(c, c, 0)
                scatter(c, c, 1)

            def turn_t(n, f, on):
                if on(2):
                    k, q, h = n - 2, (f - 2) % TRING, (f - 2) % 2
                    pool.wait_ge(s_r1, k + 1)
                    nc.gpsimd.tensor_tensor(y_t[q], y_t[q], rs1[h][:, :, :].broadcast_to([P, CJ, H]), ALU.mult).then_inc(s_u, 1)
                    pool.wait_ge(s_u, k + 1)
                    nc.gpsimd.tensor_tensor(y_t[q], y_t[q], gam[:, :, :].broadcast_to([P, CJ, H]), ALU.mult).then_inc(s_v, 1)
                if on(0):
                    q = f % TRING
                    pool.wait_ge(s_rt, n + 1)
                    if f >= TRING:
                        pool.wait_ge(s_vs, n - (TRING - 1))
                        pool.wait_ge(s_pz, n - (TRING - 1))
                    nc.gpsimd.tensor_tensor(y_t[q], agg_t[q][:, :, 0:H], rt[f % 2][:, :, :].broadcast_to([P, CJ, H]),
                                            ALU.mult).then_inc(s_t, 1)
                if on(4):
                    k, q, h = n - 4, (f - 4) % TRING, (f - 4) % 2
                    pool.wait_ge(s_r2, k + 1)
                    pool.wait_ge(s_q2, k + 1)
                    nc.gpsimd.tensor_tensor(z_t[q][:, OC:CJ, :], z_t[q][:, OC:CJ, :], rs2[h][:, OC:CJ, :].broadcast_to([P, CJ - OC, H]),
                                            ALU.mult).then_inc(s_op, 1)

            turns(pool, turn_t)

        @block.scalar
        def _(act):
            act.dma_start(srci[:, :], src_col).then_inc(s_w, 16)
            act.dma_start(z_own, z_rows).then_inc(s_w, 16)
            act.dma_start(z_bef, z_before).then_inc(s_w, 16)
            act.dma_start(wt[:, :], weight).then_inc(s_w, 16)
            act.dma_start(embs[:, :], emb_t).then_inc(s_w, 16)
            act.dma_start(adps[:, :], adapt_t).then_inc(s_w, 16)
            act.dma_start(w1s[:, :], w1).then_inc(s_w, 16)
            act.dma_start(b1s[:, :], b1).then_inc(s_w, 16)
            act.dma_start(w2s[0:H, :], w2).then_inc(s_w, 16)
            act.dma_start(w2s[H:H + 1, :], b2).then_inc(s_w, 16)
            act.dma_start(gam[:, 0, :], gamma.partition_broadcast(P).rearrange("p a k -> p (a k)")).then_inc(s_w, 16)
            act.dma_start(bet[:, 0, :], beta.partition_broadcast(P).rearrange("p a k -> p (a k)")).then_inc(s_w, 16)
            act.wait_ge(s_clear, 1)
            big = CLEAR_J * CLEAR_REP
            zeros = clear.rearrange("p (a k) -> p a k", a=1).broadcast_to([P, CLEAR_REP, CLEAR_J * S])
            for n in range(SUM_J // big):
                act.dma_start(sums.rearrange("(p j) c -> p (j c)", p=P)[:, n * big * S:(n + 1) * big * S].rearrange(
                    "p (a k) -> p a k", a=CLEAR_REP), zeros).then_inc(s_zero, 16)
            act.wait_ge(s_set, SET_PHASE)
            nc.scalar.activation(tf[:, :], ph[:, :], ACT.Sin, scale=6.283185).then_inc(s_sin, 1)
            act.wait_ge(s_w, 16 * 12)

            act.wait_ge(s_set, SET_TOTAL)

            def turn(m, f):
                c, q = m - 1, (f - 1) % 2
                if 1 <= f <= NCH:
                    act.wait_ge(s_g1, c + 1)
                    if f >= 3:
                        act.wait_ge(s_g2, c - 1)
                    nc.scalar.activation(hid[q][0:H, :], p_hid[0:H, 0:EC], ACT.Silu, bias=b1s).then_inc(s_si, 1)
                    act.wait_ge(s_bc, c + 1)
                    nc.scalar.activation(apart[q], p_type[:, 0:EC], ACT.Abs, bias=lane).then_inc(s_apart, 1)
                    act.wait_ge(s_apart, c + 1)
                    if f >= 3:
                        act.wait_ge(s_aa, c - 1)
                    nc.scalar.activation(onehot[q], apart[q], ACT.Relu, scale=-1.0, bias=1.0).then_inc(s_oh, 1)
                if f < NCH:
                    p = f % 2
                    act.wait_ge(s_row[p], nth(m, f, 2, 32))
                    if f >= 2:
                        act.wait_ge(s_look, 2 * (m - 1))
                    for k in range(ZK):
                        last = nc.scalar.activation(above[p][:, k, :], row[p], ACT.Sign, bias=edge[:, k:k + 1])
                    last.then_inc(s_ab, 1)
                if f >= 2:
                    act.wait_ge(s_ag, c)
                    if f >= 4:
                        act.wait_ge(s_sc, (c - 2) * 64)
                    nc.scalar.activation(agg[1 - q], p_agg[:, 0:C * S].rearrange("p (t k) -> p t k", k=S),
                                         ACT.Copy).then_inc(s_ev, 1)
                if 1 <= f <= NCH:
                    act.wait_ge(s_g2, c + 1)
                    act.wait_ge(s_wb, c + 1)
                    if f >= 3:
                        act.wait_ge(s_m1, c - 1)
                    for t in range(C):
                        last = nc.scalar.activation(gated[q][:, t, :], p_gate[:, t * H:(t + 1) * H], ACT.Identity,
                                                    scale=wj_a[q][:, t:t + 1], bias=wb_a[q][:, t:t + 1])
                    last.then_inc(s_gp, 1)

            chunks(act, turn)
            turn(NCH, NCH)
            turn(NCH + 1, NCH + 1)

            def scaled(k, f, a, b):
                q, h = f % TRING, f % 2
                for j in range(a, b):
                    last = nc.scalar.activation(z_t[q][:, j, :], z_t[q][:, j, :], ACT.Copy, scale=rs2[h][:, j, :])
                return last

            def turn_t(n, f, on):
                if on(5):
                    scaled(n - 5, f - 5, OA, OB)
                if on(1):
                    k, q = n - 1, (f - 1) % TRING
                    act.wait_ge(s_y, k + 1)
                    if f >= 2:
                        act.wait_ge(s_s1, k)
                    nc.scalar.activation(sq1, y_t[q], ACT.Square).then_inc(s_q1, 1)
                if on(4):
                    k = n - 4
                    act.wait_ge(s_s2, k + 1)
                    if f >= 5:
                        act.wait_ge(s_r2, k)
                    nc.scalar.activation(sd[1][:, :, :], ss[1][:, :, :], ACT.Sqrt, scale=1.0 / H, bias=eps[:, :]).then_inc(s_d2, 1)
                if on(5):
                    scaled(n - 5, f - 5, OB, OC).then_inc(s_o, 1)
                if on(1):
                    k = n - 1
                    act.wait_ge(s_s1, k + 1)
                    if f >= 2:
                        act.wait_ge(s_r1, k)
                    nc.scalar.activation(sd[0][:, :, :], ss[0][:, :, :], ACT.Sqrt, scale=1.0 / H, bias=eps[:, :]).then_inc(s_d1, 1)
                if on(4):
                    k = n - 4
                    act.wait_ge(s_r2, k + 1)
                    scaled(k, f - 4, 0, OA)
                if on(3):
                    k, q = n - 3, (f - 3) % TRING
                    act.wait_ge(s_z, k + 1)
                    if f >= 4:
                        act.wait_ge(s_s2, k)
                    nc.scalar.activation(sq2, z_t[q], ACT.Square).then_inc(s_q2, 1)

            turns(act, turn_t)

        @block.vector
        def _(dve):
            done = [0]

            def link(ins):
                done[0] += 1
                ins.then_inc(s_set, 1)
                dve.wait_ge(s_set, done[0])

            V = nc.vector
            V.memset(xc[:, NJ, :], 0.0).then_inc(s_xpad, 1)
            link(V.memset(eps[:, :], EPS))
            for q in range(2):
                link(V.memset(hid[q][0:H + 1, :], 1.0))
            dve.wait_ge(s_w, 16 * 12)
            link(V.tensor_scalar(ph[:, :], wt[:, :], 1.0 / (2 * CUTOFF), None, ALU.mult))
            link(V.tensor_copy(ti[:, :], ph[:, :]))
            link(V.tensor_copy(tf[:, :], ti[:, :]))
            link(V.scalar_tensor_tensor(ph[:, :], ph[:, :], 0.25, tf[:, :], ALU.add, ALU.subtract))
            link(V.tensor_scalar(tf[:, :], ph[:, :], 0.5, None, ALU.is_gt))
            link(V.tensor_tensor(ph[:, :], ph[:, :], tf[:, :], ALU.subtract))
            link(V.tensor_scalar(tf[:, :], ph[:, :], -0.5, None, ALU.is_lt))
            link(V.tensor_tensor(ph[:, :], ph[:, :], tf[:, :], ALU.add))
            assert done[0] == SET_PHASE
            link(V.tensor_copy(srcf[:, :], srci[:, :]))
            dve.wait_ge(s_cst, 14)
            dve.wait_ge(s_sin, 1)
            link(V.tensor_scalar(zcol[:, :], srcf[:, :], 1.0 / ZW, None, ALU.mult))
            link(V.tensor_copy(ti[:, :], zcol[:, :]))
            link(V.tensor_copy(ph[:, :], ti[:, :]))
            link(V.scalar_tensor_tensor(zcol[:, :], ph[:, :], -float(ZW), srcf[:, :], ALU.mult, ALU.add))
            link(V.tensor_scalar(ph[:, :], zcol[:, :], 0.0, float(ZW), ALU.is_lt, ALU.mult))
            link(V.tensor_tensor(zcol[:, :], zcol[:, :], ph[:, :], ALU.add))
            link(V.tensor_scalar(ph[:, :], zcol[:, :], float(ZW), float(ZW), ALU.is_ge, ALU.mult))
            link(V.tensor_tensor(zcol[:, :], zcol[:, :], ph[:, :], ALU.subtract))
            link(V.tensor_scalar(edge[:, :], edge[:, :], 0.5, None, ALU.add))
            for k in range(ZK):
                link(V.scalar_tensor_tensor(zdiff[:, k, :], z_bef[:, k, :], flip[:, k:k + 1], z_own[:, k, :], ALU.mult, ALU.add))
            link(V.tensor_tensor(trash[:, :], trash[:, :], srcf[:, :], ALU.subtract))
            link(V.reduce_sum(bsum[:, :, :], bet[:, :, :], axis=AX_X))
            link(V.scalar_tensor_tensor(bet[:, :, :], bsum[:, :, :].broadcast_to([P, 1, H]), -1.0 / H, bet[:, :, :], ALU.mult, ALU.add))
            link(V.memset(bet_k[:, :, :], 0.0))
            for n in range(3):
                link(V.tensor_copy(bet_part[:, :, :], bet[:, :, :]))
                link(V.tensor_copy(bet_k[32 * n:32 * n + 1, :, :], bet_part[32 * n:32 * n + 1, :, :]))
                if n < 2:
                    link(V.tensor_tensor(bet[:, :, :], bet[:, :, :], bet_part[:, :, :], ALU.subtract))
            link(V.tensor_scalar(tf[:, :], tf[:, :], 0.5, 0.5, ALU.mult, ALU.add))
            link(V.scalar_tensor_tensor(cw[:, :], wt[:, :], CUTOFF, tf[:, :], ALU.is_lt, ALU.mult))
            dve.wait_ge(s_vt, 1)
            link(V.tensor_copy(vts[:, :], p_hid[0:G, 0:NZ]))
            s_vts = done[0]
            dve.wait_ge(s_pair0, 1)
            link(V.tensor_copy(prest[:, :], p_pair[0:NZ, 0:NZ]))
            for n in range(3):
                link(V.tensor_copy(pair[n][:, :], prest[:, :]))
                if n < 2:
                    link(V.tensor_tensor(prest[:, :], prest[:, :], pair[n][:, :], ALU.subtract))
            assert done[0] == SET_TOTAL and s_vts == SET_VTS

            def chunk(c, f, tail=False):
                r, q = f % RING, f % 2
                if not tail:
                    for g in range(2):
                        dve.wait_ge(s_look, c * 2 + (g + 1))
                        for b in range(2):
                            t = 2 * g + b
                            last = V.scalar_tensor_tensor(found[:, t, :], nodes[:, :], zcol[:, bass.ds(c * C + t, 1)],
                                                          p_look[g][:, b * ZW:(b + 1) * ZW], ALU.is_equal, ALU.mult,
                                                          accum_out=z2[:, t:t + 1])
                        last.then_inc(s_found, 1)
                    dve.wait_ge(s_found, c * 2 + 2)
                    V.tensor_scalar(zb[q], z2[:, :], 0.5, None, ALU.mult).then_inc(s_zb, 1)
                    dve.wait_ge(s_row[q], nth(c, f, 2, 32))
                    if f >= 2:
                        dve.wait_ge(s_ag, c - 1)
                    if f >= 1:
                        dve.wait_ge(s_moved, c)
                    for g in range(2):
                        for b in range(2):
                            t = 2 * g + b
                            last = V.scalar_tensor_tensor(
                                mask[q][:, g * 3 * P + b * P:g * 3 * P + b * P + (b + 1) * P],
                                row[q][:, 2 * g * P:(2 * g + b + 1) * P], srcf[:, bass.ds(c * C + t, 1)],
                                tri[:, (1 - b) * P:2 * P], ALU.is_equal, ALU.mult, accum_out=cnt[:, t:t + 1])
                    last.then_inc(s_mask, 1)
                    if f >= PEEL:
                        lo = (c - PEEL) * CJ
                        dve.wait_ge(s_xp[f % RING], (c - f) * (16 // RING) + 16)
                        V.reduce_sum(xsum[:, 0:CJ, :], xc[:, bass.ds(lo, CJ), :], axis=AX_X).then_inc(s_xs, 1)
                    dve.wait_ge(s_mask, c + 1)
                    V.scalar_tensor_tensor(moved[:, :], cnt[:, :], 1.5, trash[:, bass.ds(c * C, C)],
                                           ALU.is_gt, ALU.mult).then_inc(s_moved, 1)
                if f >= 1:
                    pr = (f - 1) % RING
                    dve.wait_ge(s_gp, c)
                    V.tensor_tensor(msg[:, :, :], gated[1 - q][:, :, :], tg[pr][:, :, 0:H], ALU.mult).then_inc(s_m1, 1)
                if not tail:
                    if f >= PEEL:
                        dve.wait_ge(s_xs, c - (PEEL - 1))
                        V.scalar_tensor_tensor(xc[:, bass.ds(lo, CJ), :], xsum[:, 0:CJ, :].broadcast_to([P, CJ, H]), -1.0 / H,
                                               xc[:, bass.ds(lo, CJ), :], ALU.mult, ALU.add).then_inc(s_xd, 1)
                    dve.wait_ge(s_moved, c + 1)
                    if f >= RING:
                        dve.wait_ge(s_sc, (c - (RING - 1)) * 64)
                    V.tensor_tensor(idx[r][:, :], moved[:, :], srcf[:, bass.ds(c * C, C)], ALU.add).then_inc(s_idx, 1)
                if f >= 1:
                    dve.wait_ge(s_m1, c)
                    V.reduce_sum(msum[:, :, :], msg[:, :, :], axis=AX_X).then_inc(s_m2, 1)
                if not tail:
                    dve.wait_ge(s_tg[r], nth(c, f, RING, 64))
                    if f >= 2:
                        dve.wait_ge(s_gp, c - 1)
                    V.tensor_tensor(wj_a[q][:, :], cw[:, bass.ds(c * C, C)], tg[r][:, :, H], ALU.mult).then_inc(s_wj, 1)
                if f >= 1:
                    if f >= 3:
                        dve.wait_ge(s_ag, c - 2)
                    V.tensor_copy(rhs[1 - q][:, :, H], tg[pr][:, :, H])
                    dve.wait_ge(s_m2, c)
                    V.scalar_tensor_tensor(rhs[1 - q][:, :, 0:H], msum[:, :, :].broadcast_to([P, C, H]), -1.0 / H,
                                           msg[:, :, :], ALU.mult, ALU.add).then_inc(s_msg, 1)
                if not tail:
                    dve.wait_ge(s_aa, c + 1)
                    for t in range(C):
                        last = V.scalar_tensor_tensor(picked[:, t, :], types[:, :], tg[r][:, t, H + 1:H + 2].bitcast(I32),
                                                      p_pair[:, t * NZ:(t + 1) * NZ], ALU.is_equal, ALU.mult,
                                                      accum_out=adapt[:, t:t + 1])
                    last.then_inc(s_ad, 1)
                    dve.wait_ge(s_ad, c + 1)
                    V.tensor_tensor(wb_a[q][:, :], wj_a[q][:, :], adapt[:, :], ALU.mult).then_inc(s_wb, 1)

            chunks(dve, chunk)
            chunk(NCH, NCH, tail=True)
            dve.wait_ge(s_x, 32)
            lo = XLOOP
            V.reduce_sum(xsum[:, :, :], xc[:, lo:XJ, :], axis=AX_X).then_inc(s_xs, 1)
            dve.wait_ge(s_xs, NCH - PEEL + 1)
            V.scalar_tensor_tensor(xc[:, lo:XJ, :], xsum[:, :, :].broadcast_to([P, XJ - lo, H]), -1.0 / H,
                                   xc[:, lo:XJ, :], ALU.mult, ALU.add).then_inc(s_xd, 1)

            def turn_t(n, f, on):
                if on(0):
                    r = f % TRING
                    dve.wait_ge(s_agg[r], nth(n, f, TRING, 32))
                    if f >= 1:
                        dve.wait_ge(s_rt, n)
                    V.tensor_scalar(rm[:, :, :], agg_t[r][:, :, H:S], TOT_MIN, None, ALU.max).then_inc(s_rm, 1)
                    dve.wait_ge(s_rm, n + 1)
                    if f >= 2:
                        dve.wait_ge(s_t, n - 1)
                    V.reciprocal(rt[f % 2][:, :, :], rm[:, :, :]).then_inc(s_rt, 1)
                if on(1):
                    k, q = n - 1, (f - 1) % TRING
                    dve.wait_ge(s_t, k + 1)
                    V.tensor_tensor(y_t[q], y_t[q], xc[:, bass.ds(k * CJ, CJ), :], ALU.add).then_inc(s_y, 1)
                if on(4):
                    k = n - 4
                    dve.wait_ge(s_q2, k + 1)
                    if f >= 5:
                        dve.wait_ge(s_d2, k)
                    V.reduce_sum(ss[1][:, :, :], sq2, axis=AX_X).then_inc(s_s2, 1)
                if on(3):
                    k, q, h = n - 3, (f - 3) % TRING, (f - 3) % 2
                    dve.wait_ge(s_v, k + 1)
                    if f >= 5:
                        dve.wait_ge(s_z, k - 1)
                    V.reduce_sum(vsum[h][:, :, :], y_t[q], axis=AX_X).then_inc(s_vs, 1)
                if on(1):
                    k = n - 1
                    dve.wait_ge(s_q1, k + 1)
                    if f >= 2:
                        dve.wait_ge(s_d1, k)
                    V.reduce_sum(ss[0][:, :, :], sq1, axis=AX_X).then_inc(s_s1, 1)
                if on(4):
                    k, h = n - 4, (f - 4) % 2
                    dve.wait_ge(s_d2, k + 1)
                    if f >= 6:
                        dve.wait_ge(s_o, k - 1)
                        dve.wait_ge(s_op, k - 1)
                    V.reciprocal(rs2[h][:, :, :], sd[1][:, :, :]).then_inc(s_r2, 1)
                if on(3):
                    k, q, h = n - 3, (f - 3) % TRING, (f - 3) % 2
                    dve.wait_ge(s_pz, k + 1)
                    dve.wait_ge(s_vs, k + 1)
                    dve.wait_ge(s_out[q], nth(k, f - 3, TRING, 16))
                    for n_b, (a, b) in enumerate(((0, CA), (CA, CJ))):
                        last = V.scalar_tensor_tensor(z_t[q][:, a:b, :], vsum[h][:, a:b, :].broadcast_to([P, b - a, H]), -1.0 / H,
                                                      p_z[h][:, n_b, 0:(b - a) * H].rearrange("p (j k) -> p j k", k=H),
                                                      ALU.mult, ALU.add)
                    last.then_inc(s_z, 1)
                if on(1):
                    k, h = n - 1, (f - 1) % 2
                    dve.wait_ge(s_d1, k + 1)
                    if f >= 3:
                        dve.wait_ge(s_u, k - 1)
                    V.reciprocal(rs1[h][:, :, :], sd[0][:, :, :]).then_inc(s_r1, 1)

            turns(dve, turn_t)

        @block.tensor
        def _(pe):
            mm = nc.tensor.matmul
            pe.wait_ge(s_w, 16 * 12)
            mm(p_hid[0:G, 0:NZ], adps[:, :], embs[:, :], start=True, stop=True).then_inc(s_vt, 1)
            pe.wait_ge(s_set, SET_VTS)
            mm(p_pair[0:NZ, 0:NZ], embs[:, :], vts[:, :], start=True, stop=True).then_inc(s_pair0, 1)
            pe.wait_ge(s_set, SET_TOTAL)
            pe.wait_ge(s_cst, 14)

            def turn(m, f):
                c, q = m - 1, (f - 1) % 2
                if 1 <= f <= NCH:
                    pe.wait_ge(s_row[q], nth(c, f - 1, 2, 32))
                    if f >= 2:
                        pe.wait_ge(s_si, c)
                    pe.sem_inc(s_pe, 1)
                    mm(p_hid[0:H, 0:EC], w1s, att[q][0:R_ATTR, :], start=True, stop=True).then_inc(s_g1, 1)
                    pe.wait_ge(s_zb, c + 1)
                    if f >= 2:
                        pe.wait_ge(s_oh, c)
                    for t in range(C):
                        last = mm(p_type[:, t * P:(t + 1) * P], zb[q][:, t:t + 1].broadcast_to([P, P]), ident[:, :],
                                  start=True, stop=True)
                    last.then_inc(s_bc, 1)
                    pe.wait_ge(s_si, c + 1)
                    if f >= 2:
                        pe.wait_ge(s_gp, c)
                    for t in range(C):
                        last = mm(p_gate[:, t * H:(t + 1) * H], hid[q][0:H + 1, t * P:(t + 1) * P], w2s,
                                  start=True, stop=True)
                    last.then_inc(s_g2, 1)
                    pe.wait_ge(s_oh, c + 1)
                    if f >= 2:
                        pe.wait_ge(s_ad, c)
                    for t in range(C):
                        for n in range(3):
                            last = mm(p_pair[:, t * NZ:(t + 1) * NZ], onehot[q][0:NZ, t * P:(t + 1) * P], pair[n],
                                      start=(n == 0), stop=(n == 2))
                    last.then_inc(s_aa, 1)
                if f < NCH:
                    p = f % 2
                    pe.wait_ge(s_ab, m + 1)
                    for g in range(2):
                        if f >= 1:
                            pe.wait_ge(s_found, 2 * m - (1 - g))
                        for b in range(2):
                            t = 2 * g + b
                            for k in range(ZK):
                                last = mm(p_look[g][:, b * ZW:(b + 1) * ZW], above[p][:, k, t * P:(t + 1) * P],
                                          zdiff[:, k, :], start=(k == 0), stop=(k == ZK - 1))
                        last.then_inc(s_look, 1)
                if f >= 2:
                    pe.wait_ge(s_msg, c)
                    if f >= 3:
                        pe.wait_ge(s_ev, c - 1)
                    mk, v = mask[1 - q], rhs[1 - q]
                    for g in range(2):
                        o = g * 3 * P
                        t = 2 * g
                        mm(p_agg[:, t * S:(t + 1) * S], mk[:, o:o + P], v[:, t, :], start=True, stop=False)
                        mm(p_agg[:, t * S:(t + 1) * S], mk[:, o + P:o + 2 * P], v[:, t + 1, :], start=False, stop=True)
                        last = mm(p_agg[:, (t + 1) * S:(t + 2) * S], mk[:, o + 2 * P:o + 3 * P], v[:, t + 1, :],
                                  start=True, stop=True)
                    last.then_inc(s_ag, 1)

            chunks(pe, turn)
            turn(NCH, NCH)
            turn(NCH + 1, NCH + 1)

            def turn_t(n, f, on):
                if not on(2):
                    return
                k, q, h = n - 2, (f - 2) % TRING, (f - 2) % 2
                if f >= 4:
                    pe.wait_ge(s_z, k - 1)
                pe.sem_inc(s_pe, 1)
                parts = [(a, b, p_z[h][:, n_b, 0:(b - a) * H].rearrange("p (j k) -> p j k", k=H))
                         for n_b, (a, b) in enumerate(((0, CA), (CA, CJ)))]
                for a, b, o in parts:
                    mm(o, ones[:, :], bet_k[:, :, :].broadcast_to([BK, b - a, H]), start=True, stop=False)
                    mm(o, identf[:, :], xc[:, bass.ds(k * CJ + a, b - a), :], start=False, stop=False)
                pe.wait_ge(s_v, k + 1)
                pe.sem_inc(s_pe, 1)
                for a, b, o in parts:
                    last = mm(o, identf[:, :], y_t[q][:, a:b, :], start=False, stop=True)
                last.then_inc(s_pz, 1)

            turns(pe, turn_t)




def kernel(x, src, dst, edge_attr_40, edge_weight, node_type_119, node_vec, L0_gnn_W1, L0_gnn_b1, L0_gnn_W2, L0_gnn_b2,
           L0_gnn_emb, L0_gnn_adaptW, L0_gnn_gamma, L0_gnn_beta):
    import numpy as np
    import concourse.bacc as bacc
    from concourse.bass_utils import run_bass_kernel_spmd

    def padded(a, fill):
        rows = np.full((EPAD - E,) + a.shape[1:], fill, a.dtype)
        return np.concatenate([np.asarray(a), rows])

    x = np.asarray(x)
    table = np.empty((N, W), np.float32)
    table[:, 0:H] = x
    table[:, H] = np.asarray(node_vec)
    table.view(np.int32)[:, H + 1] = np.asarray(node_type_119)
    src_p = padded(src, PAD_ROW)
    dst_p = padded(dst, 0)
    z = np.concatenate([np.asarray(node_type_119), np.zeros(ZR * ZW - N, node_type_119.dtype)]).reshape(ZR, ZW)
    z_before = np.roll(z, 1, axis=0)
    arrays = {
        "in_x": x,
        "in_table": table,
        "in_src_row": src_p.reshape(NCH, EC),
        "in_cols": dst_p.reshape(NCH, C, P).transpose(0, 2, 1),
        "in_src_col": src_p.reshape(NT, P).T,
        "in_weight": padded(edge_weight, 0).reshape(NT, P).T,
        "in_attr": padded(edge_attr_40, 0).reshape(NCH, EC, R_ATTR).transpose(0, 2, 1),
        "in_z_rows": z.reshape(ZK, P, ZW).transpose(1, 0, 2),
        "in_z_before": z_before.reshape(ZK, P, ZW).transpose(1, 0, 2),
        "in_w1": np.asarray(L0_gnn_W1).T,
        "in_b1": np.asarray(L0_gnn_b1).reshape(H, 1),
        "in_w2": np.asarray(L0_gnn_W2).T,
        "in_b2": np.asarray(L0_gnn_b2).reshape(1, H),
        "in_emb_t": np.asarray(L0_gnn_emb).T,
        "in_adapt_t": np.asarray(L0_gnn_adaptW).T,
        "in_gamma": np.asarray(L0_gnn_gamma).reshape(1, H),
        "in_beta": np.asarray(L0_gnn_beta).reshape(1, H),
    }
    arrays = {k: np.ascontiguousarray(a) for k, a in arrays.items()}
    nc = bacc.Bacc("TRN2", target_bir_lowering=False, num_devices=1)
    args = [nc.dram_tensor(k, a.shape, mybir.dt.from_np(a.dtype), kind="ExternalInput").ap() for k, a in arrays.items()]
    out = nc.dram_tensor("out", (N, H), F32, kind="ExternalOutput").ap()
    gnn_resnorm(nc, *args, out)
    r = run_bass_kernel_spmd(nc, [arrays], core_ids=[0])
    return r.results[0]["out"]
```

```python
from contextlib import ExitStack

import concourse.bass as bass
from concourse import mybir

ALU = mybir.AluOpType
ACT = mybir.ActivationFunctionType
BF16 = mybir.dt.bfloat16
F32 = mybir.dt.float32
I32 = mybir.dt.int32
AX_X = mybir.AxisListType.X

P = 128
N = 100000
H = 48
E = 25000
R_ATTR = 40
NZ = 119
G = 32
CUTOFF = 6.0
EPS = 1e-5
TOT_MIN = 1e-8

C = 4
EC = C * P
A = 2
B = C // A
NCH = -(-E // EC)
EPAD = NCH * EC
NT = NCH * C
RING = 4
PEEL = RING + 1
assert (NCH - PEEL) % RING == 0

W = H + 2
S = H + 1
TRASH = N
PAD_ROW = N + 2 * P
LOADS = 11
SUM_J = 784
SUM_ROWS = P * SUM_J
CLEAR_J = 28
CLEAR_REP = 1
assert SUM_ROWS > PAD_ROW and SUM_J % (CLEAR_J * CLEAR_REP) == 0

ZK = 4
ZR = ZK * P
ZW = -(-N // ZR)

NJ = N // P
REST = N - NJ * P
XJ = NJ + 1
CJ = 17
CA = 10
TRING = 4
NST = XJ // CJ
TPEEL = 6
assert (NST - TPEEL) % TRING == 0
ARENA = 14096
BK = 65
assert NST * CJ == XJ
XLOOP = (NCH - PEEL) * CJ


LAST = 6
TRAIL = 7
OA, OB, OC = 7, 11, 14
UA = 15
SPLIT = ((0, CA), (CA, CJ))

SET_PHASE = 10
SET_VTS = 39
SET_TOTAL = 45


def gnn_resnorm(nc, x, table, src_row, cols, src_col, weight, attr, z_rows, z_before, w1, b1, w2, emb_t, adapt_t,
                gamma, beta, out):
    sums = nc.dram_tensor("sums", (SUM_ROWS, S), F32, kind="Internal").ap()
    ctx = ExitStack()
    with ctx:
        def sb(name, shape, dt):
            return ctx.enter_context(nc.sbuf_tensor(name, shape, dt))

        def sem(name):
            return ctx.enter_context(nc.semaphore(name))

        xc = sb("xc", [P, XJ, H], F32)
        arena = sb("arena", [P, ARENA], F32)
        at = [0]

        def carve(n, dt=F32, parts=P):
            size = n if dt != BF16 else -(-n // 2)
            at[0] += size
            assert at[0] <= ARENA
            a = arena[0:parts, at[0] - size:at[0]]
            return (a if dt == F32 else a.bitcast(dt))[:, 0:n]

        def carve3(j, k, dt=F32, parts=P):
            return carve(j * k, dt, parts).rearrange("p (j k) -> p j k", k=k)

        row = [carve(EC, I32) for _ in range(RING)]
        att = [carve(B * P, parts=A * R_ATTR) for _ in range(RING)]
        hid = carve(B * P, parts=A * H + 1)
        clear = carve(CLEAR_J * S)
        over = at[0]
        mask = [carve(2 * 3 * P) for _ in range(2)]
        end = at[0]
        at[0] = over
        weight_s, phase, phase_whole = carve(NT), carve(NT), carve(NT)
        whole = carve(NT, I32)
        assert at[0] <= end
        at[0] = end
        over = at[0]
        above = [carve3(ZK, EC, BF16) for _ in range(2)]
        apart = carve(EC, BF16)
        onehot = carve(EC, BF16)
        gated = carve3(C, H)
        end = at[0]
        at[0] = over
        z_own, z_bef = carve3(ZK, ZW, I32), carve3(ZK, ZW, I32)
        assert at[0] <= end
        at[0] = end
        col = [carve(C, I32) for _ in range(RING)]
        record = [carve3(C, W) for _ in range(RING)]
        sum_rows = [carve(C, I32) for _ in range(RING)]
        dst_type = carve(C, BF16)
        msg = carve3(C, H)
        centred = carve3(C, S)
        grouped_t = [carve3(C, S) for _ in range(2)]
        gate_w, gate_b = carve(C), carve(C)
        count, moved, adapt, src_type_twice = carve(C), carve(C), carve(C), carve(C)
        picked = carve3(C, NZ, BF16)
        found = carve3(C, ZW, BF16)
        msg_sum = carve3(C, 1)
        piece_sum = carve3(2 * CJ, 1)
        src_int = carve(NT, I32)
        src_f, trash, cutoff_w, place = carve(NT), carve(NT), carve(NT), carve(NT)
        zdiff = carve3(ZK, ZW, BF16)
        tri = carve(2 * P)
        ident = carve(P, BF16)
        lane = carve(1)
        flip = carve(ZK)
        edge = carve(ZK)
        types = carve(NZ)
        nodes = carve(ZW)
        w1s = carve(A * H, parts=A * R_ATTR)
        b1s = carve(1, parts=A * H)
        w2s = carve(A * H, parts=A * H + 1)
        emb_s, vts = carve(NZ, parts=G), carve(NZ, parts=G)
        adapt_s = carve(G, parts=G)
        pair = [carve(NZ, BF16, parts=NZ) for _ in range(3)]
        prest = carve(NZ, parts=NZ)

        at[0] = 0
        sums_t = [carve3(CJ, S) for _ in range(TRING)]
        y_t = [carve3(CJ, H) for _ in range(TRING)]
        out_t = [carve3(CJ, H) for _ in range(TRING)]
        sq1 = carve3(CJ, H)
        sq2 = carve3(CJ, H)

        gamma_s = sb("gamma_s", [P, 1, H], F32)
        beta_s = sb("beta_s", [P, 1, H], F32)
        beta_sum = sb("beta_sum", [P, 1, 1], F32)
        eps = sb("eps", [P, 1], F32)
        identf = sb("identf", [P, P], F32)
        mean_w = sb("mean_w", [P, P], F32)
        ones = sb("ones", [BK, P], BF16)
        beta_parts = sb("beta_parts", [BK, 1, H], BF16)
        totals = sb("totals", [P, CJ, 1], F32)
        inv_totals = [sb(f"inv_totals{n}", [P, CJ, 1], F32) for n in range(2)]
        square_sums = [sb(f"square_sums{n}", [P, CJ, 1], F32) for n in range(2)]
        deviation = [sb(f"deviation{n}", [P, CJ, 1], F32) for n in range(2)]
        inv_dev1 = [sb(f"inv_dev1_{n}", [P, CJ, 1], F32) for n in range(2)]
        inv_dev2 = [sb(f"inv_dev2_{n}", [P, CJ, 1], F32) for n in range(TRING)]
        beta_part = sb("beta_part", [P, 1, H], BF16)
        scaled_sums = [sb(f"scaled_sums{n}", [P, CJ, 1], F32) for n in range(2)]

        ps = [ctx.enter_context(nc.psum_tensor(f"ps{n}", [P, 2, 512], F32)) for n in range(4)]
        p_type, p_hid = ps[0][:, 0, :], ps[0][:, 1, :]
        p_gate, p_pair = ps[1][:, 0, :], ps[1][:, 1, :]
        p_group = ps[2][:, 0, :]
        p_look = [ps[3][:, n, :] for n in range(2)]
        p_out = ps

        weights_in = sem("weights_in")
        rest_in = sem("rest_in")
        piece_in = [sem(f"piece_in{r}") for r in range(RING)]
        table_cleared = sem("table_cleared")
        dst_in = [sem(f"dst_in{r}") for r in range(RING)]
        src_in = [sem(f"src_in{r}") for r in range(RING)]
        gathered = [sem(f"gathered{r}") for r in range(RING)]
        scattered = sem("scattered")
        sums_in = [sem(f"sums_in{r}") for r in range(TRING)]
        stored = [sem(f"stored{r}") for r in range(TRING)]
        pool_count = sem("pool_count")
        pe_count = sem("pe_count")
        zeros_ready = sem("zeros_ready")
        consts_ready = sem("consts_ready")
        pad_ready = sem("pad_ready")
        setup_steps = sem("setup_steps")
        vt_ready = sem("vt_ready")
        pair_table_ready = sem("pair_table_ready")
        sine_ready = sem("sine_ready")
        compared = sem("compared")
        looked_up = sem("looked_up")
        src_type_found = sem("src_type_found")
        dst_type_ready = sem("dst_type_ready")
        dst_type_spread = sem("dst_type_spread")
        apart_ready = sem("apart_ready")
        onehot_ready = sem("onehot_ready")
        pair_rows_ready = sem("pair_rows_ready")
        adapt_ready = sem("adapt_ready")
        layer1_ready = sem("layer1_ready")
        hidden_ready = sem("hidden_ready")
        layer2_ready = sem("layer2_ready")
        gate_w_ready = sem("gate_w_ready")
        gate_b_ready = sem("gate_b_ready")
        gates_ready = sem("gates_ready")
        masks_ready = sem("masks_ready")
        moved_ready = sem("moved_ready")
        sum_rows_ready = sem("sum_rows_ready")
        products_ready = sem("products_ready")
        product_sums_ready = sem("product_sums_ready")
        messages_ready = sem("messages_ready")
        grouped = sem("grouped")
        grouped_in_sbuf = sem("grouped_in_sbuf")
        piece_summed = sem("piece_summed")
        piece_centred = sem("piece_centred")
        totals_ready = sem("totals_ready")
        inv_totals_ready = sem("inv_totals_ready")
        means_ready = sem("means_ready")
        residual_ready = sem("residual_ready")
        squares1_ready = sem("squares1_ready")
        square_sums1_ready = sem("square_sums1_ready")
        deviation1_ready = sem("deviation1_ready")
        inv_deviation1_ready = sem("inv_deviation1_ready")
        normed_by_pool = sem("normed_by_pool")
        normed_by_dve = sem("normed_by_dve")
        scaled_ready = sem("scaled_ready")
        scaled_sums_ready = sem("scaled_sums_ready")
        scaled_added = sem("scaled_added")
        centred_ready = sem("centred_ready")
        squares2_ready = sem("squares2_ready")
        square_sums2_ready = sem("square_sums2_ready")
        deviation2_ready = sem("deviation2_ready")
        inv_deviation2_ready = sem("inv_deviation2_ready")
        out_by_act = sem("out_by_act")
        out_by_dve = sem("out_by_dve")

        block = ctx.enter_context(nc.Block())

        def chunks(eng, body, start=PEEL, end=NCH):
            for c in range(start):
                body(c, c)
            assert start >= PEEL - 1 and (end - start) % RING == 0
            with eng.Fori(0, (end - start) // RING) as i:
                for k in range(RING):
                    body(i * RING + (start + k), start + k)

        def nth(c, first, ring, each):
            if isinstance(c, int):
                return (c // ring + 1) * each
            return (c - first % ring) * (each // ring) + each

        def row_out(q, a, b):
            n = int(a >= CA)
            return p_out[q][:, n, (a - n * CA) * H:(b - n * CA) * H].rearrange("p (j k) -> p j k", k=H)

        def turns(eng, body):
            for n in range(TPEEL):
                body(n, n, lambda lag, n=n: n >= lag)
            with eng.Fori(0, (NST - TPEEL) // TRING) as i:
                for k in range(TRING):
                    body(i * TRING + (TPEEL + k), TPEEL + k, lambda lag: True)
            for n in range(NST, NST + LAST):
                body(n, n, lambda lag, n=n: n - lag < NST)

        @block.sync
        def _(sp):
            x_v = x[0:NJ * P, :].rearrange("(p j) c -> p j c", p=P)
            for r in range(TRING):
                sp.sem_inc(stored[r], 16)

            def load(m, f, ahead=True):
                if ahead:
                    r = f % RING
                    if f >= RING:
                        sp.wait_ge(gathered[r], nth(m, f, RING, 64) - 64)
                    sp.dma_start(col[r][:, :], cols[bass.ds(m, 1)].rearrange("a p k -> (a p) k")).then_inc(dst_in[r], 16)
                if f >= 1:
                    c, r = m - 1, (f - 1) % RING
                    if f > RING:
                        sp.wait_ge(masks_ready, c - (RING - 1))
                        sp.wait_ge(compared, c - (RING - 1))
                        sp.wait_ge(layer1_ready, c - (RING - 1))
                    sp.dma_start(row[r][:, :], src_row[bass.ds(c, 1), :].partition_broadcast(P).rearrange(
                        "p a k -> p (a k)")).then_inc(src_in[r], 16)
                    sp.dma_start(att[r], attr[bass.ds(c, 1)].rearrange("a r k -> (a r) k")).then_inc(src_in[r], 16)
                if ahead and f >= PEEL:
                    lo = (m - PEEL) * CJ
                    sp.dma_start(xc[:, bass.ds(lo, CJ), :], x_v[:, bass.ds(lo, CJ), :]).then_inc(piece_in[f % RING], 16)

            chunks(sp, load)
            load(NCH, NCH, ahead=False)
            sp.wait_ge(pad_ready, 1)
            sp.dma_start(xc[:, XLOOP:NJ, :], x_v[:, XLOOP:NJ, :]).then_inc(rest_in, 16)
            sp.dma_start(xc[0:REST, NJ, :], x[NJ * P:N, :]).then_inc(rest_in, 16)

            sums_v = sums[0:NJ * P, :].rearrange("(p j) c -> p j c", p=P)
            out_v = out[0:NJ * P, :].rearrange("(p j) c -> p j c", p=P)
            sp.wait_ge(scattered, NCH * 64)
            sp.wait_ge(gates_ready, NCH)
            sp.wait_ge(grouped, NCH)

            def fetch(k, f):
                q = f % TRING
                if f >= TRING:
                    sp.wait_ge(means_ready, k - (TRING - 1))
                for a, b in ((0, CJ // 2), (CJ // 2, CJ)):
                    sp.dma_start(sums_t[q][:, a:b, :], sums_v[:, bass.ds(k * CJ + a, b - a), :]).then_inc(sums_in[q], 16)

            def store(k, f):
                sp.wait_ge(out_by_act, k + 1)
                sp.wait_ge(out_by_dve, k + 1)
                sp.dma_start(out_v[:, bass.ds(k * CJ, CJ), :], out_t[f % TRING]).then_inc(stored[f % TRING], 16)

            first = TRAIL + 2
            for k in range(first):
                fetch(k, k)
                if k >= TRAIL:
                    store(k - TRAIL, k - TRAIL)
            last = NST - 1
            assert (last - first) % TRING == 0
            with sp.Fori(0, (last - first) // TRING) as i:
                for k in range(TRING):
                    fetch(i * TRING + (first + k), first + k)
                    store(i * TRING + (first + k - TRAIL), first + k - TRAIL)
            q = last % TRING
            sp.wait_ge(means_ready, last - (TRING - 1))
            sp.dma_start(sums_t[q][:, 0:CJ - 1, :], sums_v[:, last * CJ:NJ, :]).then_inc(sums_in[q], 16)
            sp.dma_start(sums_t[q][0:REST, CJ - 1, :], sums[NJ * P:N, :]).then_inc(sums_in[q], 16)
            for k in range(last - TRAIL, last):
                store(k, k)
            sp.wait_ge(out_by_act, NST)
            sp.wait_ge(out_by_dve, NST)
            sp.dma_start(out_v[:, last * CJ:NJ, :], out_t[q][:, 0:CJ - 1, :]).then_inc(stored[q], 16)
            sp.dma_start(out[NJ * P:N, :], out_t[q][0:REST, CJ - 1, :]).then_inc(stored[q], 16)
            for r in range(TRING):
                sp.wait_ge(stored[r], 16 * (1 + len(range(r, NST, TRING)) + (r == q)))

        @block.gpsimd
        def _(pool):
            nc.gpsimd.memset(clear, 0.0).then_inc(zeros_ready, 1)
            nc.gpsimd.memset(tri[:, :], 1.0).then_inc(consts_ready, 1)
            nc.gpsimd.memset(ident[:, :], 0.0).then_inc(consts_ready, 1)
            nc.gpsimd.iota(lane[:, :], [[0, 1]], base=0, channel_multiplier=-1,
                           allow_small_or_imprecise_dtypes=True).then_inc(consts_ready, 1)
            nc.gpsimd.iota(types[:, :], [[2, NZ]], base=0, channel_multiplier=0,
                           allow_small_or_imprecise_dtypes=True).then_inc(consts_ready, 1)
            nc.gpsimd.iota(trash[:, :].rearrange("p (g b) -> p g b", b=2), [[0, NT // 2], [P, 2]], base=TRASH,
                           channel_multiplier=1, allow_small_or_imprecise_dtypes=True).then_inc(consts_ready, 1)
            nc.gpsimd.iota(nodes[:, :], [[1, ZW]], base=0, channel_multiplier=0,
                           allow_small_or_imprecise_dtypes=True).then_inc(consts_ready, 1)
            nc.gpsimd.iota(edge[:, :], [[-P * ZW, ZK]], base=0, channel_multiplier=-ZW,
                           allow_small_or_imprecise_dtypes=True).then_inc(consts_ready, 1)
            nc.gpsimd.memset(flip[:, :], -1.0).then_inc(consts_ready, 1)
            nc.gpsimd.memset(identf[:, :], 0.0).then_inc(consts_ready, 1)
            nc.gpsimd.memset(mean_w[:, :], 0.0).then_inc(consts_ready, 1)
            nc.gpsimd.memset(ones[:, :], 1.0).then_inc(consts_ready, 1)
            pool.wait_ge(consts_ready, 11)
            nc.gpsimd.affine_select(out=identf[:, :], in_=identf[:, :], compare_op=ALU.not_equal, fill=1.0,
                                    base=0, pattern=[[-1, P]], channel_multiplier=1).then_inc(consts_ready, 1)
            nc.gpsimd.affine_select(out=mean_w[:, :], in_=mean_w[:, :], compare_op=ALU.not_equal, fill=-1.0 / H,
                                    base=0, pattern=[[-1, P]], channel_multiplier=1).then_inc(consts_ready, 1)
            nc.gpsimd.affine_select(out=flip[:, :], in_=flip[:, :], compare_op=ALU.not_equal, fill=1.0,
                                    base=0, pattern=[[P, ZK]], channel_multiplier=1).then_inc(consts_ready, 1)
            nc.gpsimd.affine_select(out=tri[:, P:2 * P], in_=tri[:, P:2 * P], compare_op=ALU.is_ge, fill=0.0,
                                    base=0, pattern=[[-1, P]], channel_multiplier=1).then_inc(consts_ready, 1)
            nc.gpsimd.affine_select(out=ident[:, :], in_=ident[:, :], compare_op=ALU.not_equal, fill=1.0,
                                    base=0, pattern=[[-1, P]], channel_multiplier=1).then_inc(consts_ready, 1)

            def gather(c, f, ts):
                r = f % RING
                if 0 in ts:
                    pool.wait_ge(dst_in[r], nth(c, f, RING, 16))
                    if f >= RING:
                        pool.wait_ge(messages_ready, c - (RING - 1))
                pool.sem_inc(pool_count, 1)
                for t in ts:
                    pool.indirect_dma_start(record[r][:, t, :], None, table, bass.IndirectOffsetOnAxis(
                        ap=col[r][:, t:t + 1], axis=0)).then_inc(gathered[r], 16)

            def scatter(c, f, g):
                r, q = f % RING, f % 2
                if g == 0:
                    pool.wait_ge(grouped_in_sbuf, c + 1)
                    pool.wait_ge(sum_rows_ready, c + 1)
                if not (f == 0 and g == 0):
                    pool.wait_ge(scattered, c * 64 + 32 * g)
                else:
                    pool.wait_ge(table_cleared, 16 * (SUM_J // (CLEAR_J * CLEAR_REP)))
                pool.sem_inc(pool_count, 1)
                for t in (2 * g, 2 * g + 1):
                    pool.indirect_dma_start(sums, bass.IndirectOffsetOnAxis(ap=sum_rows[r][:, t:t + 1], axis=0),
                                            grouped_t[q][:, t, :], None, compute_op=ALU.add).then_inc(scattered, 16)

            LAG = 4

            def turn(c, f):
                gather(c, f, (0, 1))
                if f >= LAG:
                    scatter(c - LAG, f - LAG, 0)
                gather(c, f, (2, 3))
                if f >= LAG:
                    scatter(c - LAG, f - LAG, 1)

            chunks(pool, turn)
            for c in range(NCH - LAG, NCH):
                scatter(c, c, 0)
                scatter(c, c, 1)

            def turn_t(n, f, on):
                if on(3):
                    k, q = n - 3, (f - 3) % TRING
                    pool.wait_ge(normed_by_pool, k + 1)
                    pool.wait_ge(normed_by_dve, k + 1)
                    nc.gpsimd.tensor_tensor(y_t[q], y_t[q], gamma_s[:, :, :].broadcast_to([P, CJ, H]),
                                            ALU.mult).then_inc(scaled_ready, 1)
                if on(2):
                    k, q, h = n - 2, (f - 2) % TRING, (f - 2) % 2
                    pool.wait_ge(inv_deviation1_ready, k + 1)
                    nc.gpsimd.tensor_tensor(y_t[q][:, 0:UA, :], y_t[q][:, 0:UA, :],
                                            inv_dev1[h][:, 0:UA, :].broadcast_to([P, UA, H]),
                                            ALU.mult).then_inc(normed_by_pool, 1)
                if on(0):
                    q = f % TRING
                    pool.wait_ge(inv_totals_ready, n + 1)
                    if f >= TRING:
                        pool.wait_ge(scaled_sums_ready, n - (TRING - 1))
                        pool.wait_ge(scaled_added, n - (TRING - 1))
                    nc.gpsimd.tensor_tensor(y_t[q], sums_t[q][:, :, 0:H], inv_totals[f % 2][:, :, :].broadcast_to([P, CJ, H]),
                                            ALU.mult).then_inc(means_ready, 1)

            turns(pool, turn_t)

        @block.scalar
        def _(act):
            big = CLEAR_J * CLEAR_REP
            zeros = clear.rearrange("p (a k) -> p a k", a=1).broadcast_to([P, CLEAR_REP, CLEAR_J * S])

            def zero(n):
                act.dma_start(sums.rearrange("(p j) c -> p (j c)", p=P)[:, n * big * S:(n + 1) * big * S].rearrange(
                    "p (a k) -> p a k", a=CLEAR_REP), zeros).then_inc(table_cleared, 16)

            act.dma_start(src_int[:, :], src_col).then_inc(weights_in, 16)
            act.dma_start(weight_s[:, :], weight).then_inc(weights_in, 16)
            act.wait_ge(zeros_ready, 1)
            for n in range(2):
                zero(n)
            act.dma_start(emb_s[:, :], emb_t).then_inc(weights_in, 16)
            act.dma_start(adapt_s[:, :], adapt_t).then_inc(weights_in, 16)
            act.dma_start(z_own, z_rows).then_inc(weights_in, 16)
            act.dma_start(z_bef, z_before).then_inc(weights_in, 16)
            act.dma_start(w1s[:, :], w1).then_inc(weights_in, 16)
            act.dma_start(b1s[:, :], b1).then_inc(weights_in, 16)
            act.dma_start(w2s[:, :], w2).then_inc(weights_in, 16)
            act.dma_start(gamma_s[:, 0, :], gamma.partition_broadcast(P).rearrange("p a k -> p (a k)")).then_inc(weights_in, 16)
            act.dma_start(beta_s[:, 0, :], beta.partition_broadcast(P).rearrange("p a k -> p (a k)")).then_inc(weights_in, 16)
            for n in range(2, SUM_J // big):
                zero(n)
            act.wait_ge(setup_steps, SET_PHASE)
            nc.scalar.activation(phase_whole[:, :], phase[:, :], ACT.Sin, scale=6.283185).then_inc(sine_ready, 1)
            act.wait_ge(weights_in, 16 * LOADS)

            act.wait_ge(setup_steps, SET_TOTAL)

            def compare(c, f, ks):
                if 0 in ks:
                    act.wait_ge(src_in[f % RING], nth(c, f, RING, 32))
                    if f >= 2:
                        act.wait_ge(looked_up, 2 * (c - 1))
                for k in ks:
                    last = nc.scalar.activation(above[f % 2][:, k, :], row[f % RING], ACT.Sign, bias=edge[:, k:k + 1])
                if ZK - 1 in ks:
                    last.then_inc(compared, 1)

            def one_hot(c, f):
                act.wait_ge(dst_type_spread, c + 1)
                nc.scalar.activation(apart, p_type[:, 0:EC], ACT.Abs, bias=lane).then_inc(apart_ready, 1)
                act.wait_ge(apart_ready, c + 1)
                if f >= 1:
                    act.wait_ge(pair_rows_ready, c)
                nc.scalar.activation(onehot, apart, ACT.Relu, scale=-1.0, bias=1.0).then_inc(onehot_ready, 1)

            def layer(c, f):
                act.wait_ge(layer1_ready, c + 1)
                if f >= 1:
                    act.wait_ge(layer2_ready, c)
                nc.scalar.activation(hid[0:A * H, :], p_hid[0:A * H, 0:B * P], ACT.Silu, bias=b1s).then_inc(hidden_ready, 1)

            def gates(c, f):
                act.wait_ge(layer2_ready, c + 1)
                act.wait_ge(gate_b_ready, c + 1)
                if f >= 1:
                    act.wait_ge(products_ready, c)
                for t in range(C):
                    last = nc.scalar.activation(gated[:, t, :], p_gate[:, t * H:(t + 1) * H], ACT.Identity,
                                                scale=gate_w[:, t:t + 1], bias=gate_b[:, t:t + 1])
                last.then_inc(gates_ready, 1)

            def evacuate(c, f):
                act.wait_ge(grouped, c + 1)
                if f >= 2:
                    act.wait_ge(scattered, (c - 1) * 64)
                nc.scalar.activation(grouped_t[f % 2], p_group[:, 0:C * S].rearrange("p (t k) -> p t k", k=S),
                                     ACT.Copy).then_inc(grouped_in_sbuf, 1)

            def turn(c, f, more=True):
                if more:
                    compare(c + 1, f + 1, (0, 1))
                    one_hot(c + 1, f + 1)
                    layer(c + 1, f + 1)
                    compare(c + 1, f + 1, (2,))
                gates(c, f)
                if f >= 1:
                    evacuate(c - 1, f - 1)
                if more:
                    compare(c + 1, f + 1, (3,))

            compare(0, 0, range(ZK))
            one_hot(0, 0)
            layer(0, 0)
            chunks(act, turn, PEEL - 1, NCH - 1)
            turn(NCH - 1, NCH - 1, more=False)
            evacuate(NCH - 1, NCH - 1)

            def scaled(k, f, a, b):
                q = f % TRING
                for j in range(a, b):
                    last = nc.scalar.activation(out_t[q][:, j, :], row_out(q, j, j + 1)[:, 0, :], ACT.Copy,
                                                scale=inv_dev2[q][:, j, :])
                return last

            def turn_t(n, f, on):
                if on(6):
                    act.wait_ge(inv_deviation2_ready, n - 5)
                    scaled(n - 6, f - 6, 0, OA)
                if on(2):
                    k = n - 2
                    act.wait_ge(square_sums1_ready, k + 1)
                    if f >= 3:
                        act.wait_ge(inv_deviation1_ready, k)
                    nc.scalar.activation(deviation[0][:, :, :], square_sums[0][:, :, :], ACT.Sqrt, scale=1.0 / H,
                                         bias=eps[:, :]).then_inc(deviation1_ready, 1)
                if on(6):
                    act.wait_ge(out_by_dve, n - 5)
                    scaled(n - 6, f - 6, OA, OB)
                if on(5):
                    k = n - 5
                    act.wait_ge(square_sums2_ready, k + 1)
                    if f >= 6:
                        act.wait_ge(inv_deviation2_ready, k)
                    nc.scalar.activation(deviation[1][:, :, :], square_sums[1][:, :, :], ACT.Sqrt, scale=1.0 / H,
                                         bias=eps[:, :]).then_inc(deviation2_ready, 1)
                if on(4):
                    k, q = n - 4, (f - 4) % TRING
                    act.wait_ge(centred_ready, k + 1)
                    if f >= 5:
                        act.wait_ge(square_sums2_ready, k)
                    for a, b in SPLIT:
                        last = nc.scalar.activation(sq2[:, a:b, :], row_out(q, a, b), ACT.Square)
                    last.then_inc(squares2_ready, 1)
                if on(6):
                    scaled(n - 6, f - 6, OB, OC).then_inc(out_by_act, 1)
                if on(1):
                    k, q = n - 1, (f - 1) % TRING
                    act.wait_ge(residual_ready, k + 1)
                    if f >= 2:
                        act.wait_ge(square_sums1_ready, k)
                    nc.scalar.activation(sq1, y_t[q], ACT.Square).then_inc(squares1_ready, 1)

            turns(act, turn_t)

        @block.vector
        def _(dve):
            done = [0]

            def link(ins):
                done[0] += 1
                ins.then_inc(setup_steps, 1)
                dve.wait_ge(setup_steps, done[0])

            V = nc.vector
            V.memset(xc[:, NJ, :], 0.0).then_inc(pad_ready, 1)
            link(V.memset(eps[:, :], EPS))
            link(V.memset(hid, 1.0))
            dve.wait_ge(weights_in, 16 * LOADS)
            link(V.tensor_scalar(phase[:, :], weight_s[:, :], 1.0 / (2 * CUTOFF), None, ALU.mult))
            link(V.tensor_copy(whole[:, :], phase[:, :]))
            link(V.tensor_copy(phase_whole[:, :], whole[:, :]))
            link(V.scalar_tensor_tensor(phase[:, :], phase[:, :], 0.25, phase_whole[:, :], ALU.add, ALU.subtract))
            link(V.tensor_scalar(phase_whole[:, :], phase[:, :], 0.5, None, ALU.is_gt))
            link(V.tensor_tensor(phase[:, :], phase[:, :], phase_whole[:, :], ALU.subtract))
            link(V.tensor_scalar(phase_whole[:, :], phase[:, :], -0.5, None, ALU.is_lt))
            link(V.tensor_tensor(phase[:, :], phase[:, :], phase_whole[:, :], ALU.add))
            assert done[0] == SET_PHASE
            link(V.tensor_copy(src_f[:, :], src_int[:, :]))
            dve.wait_ge(consts_ready, 16)
            dve.wait_ge(sine_ready, 1)
            link(V.tensor_scalar(place[:, :], src_f[:, :], 1.0 / ZW, None, ALU.mult))
            link(V.tensor_copy(whole[:, :], place[:, :]))
            link(V.tensor_copy(phase[:, :], whole[:, :]))
            link(V.scalar_tensor_tensor(place[:, :], phase[:, :], -float(ZW), src_f[:, :], ALU.mult, ALU.add))
            link(V.tensor_scalar(phase[:, :], place[:, :], 0.0, float(ZW), ALU.is_lt, ALU.mult))
            link(V.tensor_tensor(place[:, :], place[:, :], phase[:, :], ALU.add))
            link(V.tensor_scalar(phase[:, :], place[:, :], float(ZW), float(ZW), ALU.is_ge, ALU.mult))
            link(V.tensor_tensor(place[:, :], place[:, :], phase[:, :], ALU.subtract))
            link(V.tensor_scalar(edge[:, :], edge[:, :], 0.5, None, ALU.add))
            for k in range(ZK):
                link(V.scalar_tensor_tensor(zdiff[:, k, :], z_bef[:, k, :], flip[:, k:k + 1], z_own[:, k, :], ALU.mult, ALU.add))
            link(V.tensor_tensor(trash[:, :], trash[:, :], src_f[:, :], ALU.subtract))
            link(V.reduce_sum(beta_sum[:, :, :], beta_s[:, :, :], axis=AX_X))
            link(V.scalar_tensor_tensor(beta_s[:, :, :], beta_sum[:, :, :].broadcast_to([P, 1, H]), -1.0 / H,
                                        beta_s[:, :, :], ALU.mult, ALU.add))
            link(V.memset(beta_parts[:, :, :], 0.0))
            for n in range(3):
                link(V.tensor_copy(beta_part[:, :, :], beta_s[:, :, :]))
                link(V.tensor_copy(beta_parts[32 * n:32 * n + 1, :, :], beta_part[32 * n:32 * n + 1, :, :]))
                if n < 2:
                    link(V.tensor_tensor(beta_s[:, :, :], beta_s[:, :, :], beta_part[:, :, :], ALU.subtract))
            link(V.tensor_scalar(phase_whole[:, :], phase_whole[:, :], 0.5, 0.5, ALU.mult, ALU.add))
            link(V.scalar_tensor_tensor(cutoff_w[:, :], weight_s[:, :], CUTOFF, phase_whole[:, :], ALU.is_lt, ALU.mult))
            dve.wait_ge(vt_ready, 1)
            link(V.tensor_copy(vts[:, :], p_hid[0:G, 0:NZ]))
            s_vts = done[0]
            dve.wait_ge(pair_table_ready, 1)
            link(V.tensor_copy(prest[:, :], p_pair[0:NZ, 0:NZ]))
            for n in range(3):
                link(V.tensor_copy(pair[n][:, :], prest[:, :]))
                if n < 2:
                    link(V.tensor_tensor(prest[:, :], prest[:, :], pair[n][:, :], ALU.subtract))
            assert done[0] == SET_TOTAL and s_vts == SET_VTS

            def partner(c, f):
                dve.wait_ge(gathered[f % RING], nth(c, f, RING, 64))
                if f >= 1:
                    dve.wait_ge(dst_type_spread, c)
                V.tensor_copy(dst_type, record[f % RING][:, :, H + 1].bitcast(I32)).then_inc(dst_type_ready, 1)

            def select(c, f, g):
                dve.wait_ge(looked_up, c * 2 + (g + 1))
                for b in range(2):
                    t = 2 * g + b
                    last = V.scalar_tensor_tensor(found[:, t, :], nodes[:, :], place[:, bass.ds(c * C + t, 1)],
                                                  p_look[g][:, b * ZW:(b + 1) * ZW], ALU.is_equal, ALU.mult,
                                                  accum_out=src_type_twice[:, t:t + 1])
                last.then_inc(src_type_found, 1)

            def compare(c, f, g):
                q, r = f % 2, f % RING
                if g == 0:
                    dve.wait_ge(src_in[r], nth(c, f, RING, 32))
                    if f >= 2:
                        dve.wait_ge(grouped, c - 1)
                    if f >= 1:
                        dve.wait_ge(moved_ready, c)
                for b in range(2):
                    t = 2 * g + b
                    last = V.scalar_tensor_tensor(
                        mask[q][:, g * 3 * P + b * P:g * 3 * P + b * P + (b + 1) * P],
                        row[r][:, 2 * g * P:(2 * g + b + 1) * P], src_f[:, bass.ds(c * C + t, 1)],
                        tri[:, (1 - b) * P:2 * P], ALU.is_equal, ALU.mult, accum_out=count[:, t:t + 1])
                if g == 1:
                    last.then_inc(masks_ready, 1)

            def chunk(c, f, more=True):
                r = f % RING
                if more:
                    partner(c + 1, f + 1)
                select(c, f, 0)
                compare(c, f, 0)
                select(c, f, 1)
                dve.wait_ge(pair_rows_ready, c + 1)
                dve.wait_ge(src_type_found, c * 2 + 2)
                for t in range(C):
                    last = V.scalar_tensor_tensor(picked[:, t, :], types[:, :], src_type_twice[:, t:t + 1],
                                                  p_pair[:, t * NZ:(t + 1) * NZ], ALU.is_equal, ALU.mult,
                                                  accum_out=adapt[:, t:t + 1])
                last.then_inc(adapt_ready, 1)
                if f >= 1:
                    dve.wait_ge(gates_ready, c)
                V.tensor_tensor(gate_w[:, :], cutoff_w[:, bass.ds(c * C, C)], record[r][:, :, H],
                                ALU.mult).then_inc(gate_w_ready, 1)
                dve.wait_ge(gate_w_ready, c + 1)
                dve.wait_ge(adapt_ready, c + 1)
                V.tensor_tensor(gate_b[:, :], gate_w[:, :], adapt[:, :], ALU.mult).then_inc(gate_b_ready, 1)
                piece = f >= PEEL - 1 and more
                if piece:
                    lo = (c - (PEEL - 1)) * CJ
                    dve.wait_ge(piece_in[(f + 1) % RING], (c - f) * (16 // RING) + 16)
                    V.reduce_sum(piece_sum[:, 0:CJ, :], xc[:, bass.ds(lo, CJ), :], axis=AX_X).then_inc(piece_summed, 1)
                compare(c, f, 1)
                dve.wait_ge(masks_ready, c + 1)
                V.scalar_tensor_tensor(moved[:, :], count[:, :], 1.5, trash[:, bass.ds(c * C, C)],
                                       ALU.is_gt, ALU.mult).then_inc(moved_ready, 1)
                dve.wait_ge(gates_ready, c + 1)
                V.tensor_tensor(msg[:, :, :], gated[:, :, :], record[r][:, :, 0:H], ALU.mult).then_inc(products_ready, 1)
                dve.wait_ge(moved_ready, c + 1)
                if f >= RING:
                    dve.wait_ge(scattered, (c - (RING - 1)) * 64)
                V.tensor_tensor(sum_rows[r][:, :], moved[:, :], src_f[:, bass.ds(c * C, C)], ALU.add).then_inc(sum_rows_ready, 1)
                if f >= 1:
                    dve.wait_ge(grouped, c)
                V.tensor_copy(centred[:, :, H], record[r][:, :, H])
                dve.wait_ge(products_ready, c + 1)
                V.reduce_sum(msg_sum[:, :, :], msg[:, :, :], axis=AX_X).then_inc(product_sums_ready, 1)
                if piece:
                    dve.wait_ge(piece_summed, c - (PEEL - 2))
                    V.scalar_tensor_tensor(xc[:, bass.ds(lo, CJ), :], piece_sum[:, 0:CJ, :].broadcast_to([P, CJ, H]), -1.0 / H,
                                           xc[:, bass.ds(lo, CJ), :], ALU.mult, ALU.add).then_inc(piece_centred, 1)
                dve.wait_ge(product_sums_ready, c + 1)
                V.scalar_tensor_tensor(centred[:, :, 0:H], msg_sum[:, :, :].broadcast_to([P, C, H]), -1.0 / H,
                                       msg[:, :, :], ALU.mult, ALU.add).then_inc(messages_ready, 1)

            partner(0, 0)
            chunks(dve, chunk, PEEL - 1, NCH - 1)
            chunk(NCH - 1, NCH - 1, more=False)
            dve.wait_ge(rest_in, 32)
            lo = XLOOP
            V.reduce_sum(piece_sum[:, :, :], xc[:, lo:XJ, :], axis=AX_X).then_inc(piece_summed, 1)
            dve.wait_ge(piece_summed, NCH - PEEL + 1)
            V.scalar_tensor_tensor(xc[:, lo:XJ, :], piece_sum[:, :, :].broadcast_to([P, XJ - lo, H]), -1.0 / H,
                                   xc[:, lo:XJ, :], ALU.mult, ALU.add).then_inc(piece_centred, 1)

            def turn_t(n, f, on):
                if on(4):
                    k, q, h = n - 4, (f - 4) % TRING, (f - 4) % 2
                    dve.wait_ge(scaled_ready, k + 1)
                    if f >= 6:
                        dve.wait_ge(centred_ready, k - 1)
                    V.reduce_sum(scaled_sums[h][:, :, :], y_t[q], axis=AX_X).then_inc(scaled_sums_ready, 1)
                if on(2):
                    k = n - 2
                    dve.wait_ge(squares1_ready, k + 1)
                    if f >= 3:
                        dve.wait_ge(deviation1_ready, k)
                    V.reduce_sum(square_sums[0][:, :, :], sq1, axis=AX_X).then_inc(square_sums1_ready, 1)
                if on(5):
                    k = n - 5
                    dve.wait_ge(squares2_ready, k + 1)
                    if f >= 6:
                        dve.wait_ge(deviation2_ready, k)
                    V.reduce_sum(square_sums[1][:, :, :], sq2, axis=AX_X).then_inc(square_sums2_ready, 1)
                if on(2):
                    k, h = n - 2, (f - 2) % 2
                    dve.wait_ge(deviation1_ready, k + 1)
                    if f >= 4:
                        dve.wait_ge(normed_by_pool, k - 1)
                    V.reciprocal(inv_dev1[h][:, :, :], deviation[0][:, :, :]).then_inc(inv_deviation1_ready, 1)
                if on(0):
                    r = f % TRING
                    dve.wait_ge(sums_in[r], nth(n, f, TRING, 32))
                    if f >= 1:
                        dve.wait_ge(inv_totals_ready, n)
                    V.tensor_scalar(totals[:, :, :], sums_t[r][:, :, H:S], TOT_MIN, None, ALU.max).then_inc(totals_ready, 1)
                if on(2):
                    k, q, h = n - 2, (f - 2) % TRING, (f - 2) % 2
                    dve.wait_ge(inv_deviation1_ready, k + 1)
                    V.tensor_tensor(y_t[q][:, UA:CJ, :], y_t[q][:, UA:CJ, :],
                                    inv_dev1[h][:, UA:CJ, :].broadcast_to([P, CJ - UA, H]),
                                    ALU.mult).then_inc(normed_by_dve, 1)
                if on(0):
                    dve.wait_ge(totals_ready, n + 1)
                    if f >= 2:
                        dve.wait_ge(means_ready, n - 1)
                    V.reciprocal(inv_totals[f % 2][:, :, :], totals[:, :, :]).then_inc(inv_totals_ready, 1)
                if on(5):
                    k, q = n - 5, (f - 5) % TRING
                    dve.wait_ge(deviation2_ready, k + 1)
                    dve.wait_ge(stored[q], nth(k, f - 5, TRING, 16))
                    V.reciprocal(inv_dev2[q][:, :, :], deviation[1][:, :, :]).then_inc(inv_deviation2_ready, 1)
                if on(1):
                    k, q = n - 1, (f - 1) % TRING
                    dve.wait_ge(means_ready, k + 1)
                    V.tensor_tensor(y_t[q], y_t[q], xc[:, bass.ds(k * CJ, CJ), :], ALU.add).then_inc(residual_ready, 1)
                if on(5):
                    k, q = n - 5, (f - 5) % TRING
                    dve.wait_ge(inv_deviation2_ready, k + 1)
                    V.tensor_tensor(out_t[q][:, OC:CJ, :], row_out(q, OC, CJ),
                                    inv_dev2[q][:, OC:CJ, :].broadcast_to([P, CJ - OC, H]),
                                    ALU.mult).then_inc(out_by_dve, 1)

            turns(dve, turn_t)

        @block.tensor
        def _(pe):
            mm = nc.tensor.matmul
            pe.wait_ge(weights_in, 16 * LOADS)
            mm(p_hid[0:G, 0:NZ], adapt_s[:, :], emb_s[:, :], start=True, stop=True).then_inc(vt_ready, 1)
            pe.wait_ge(setup_steps, SET_VTS)
            mm(p_pair[0:NZ, 0:NZ], vts[:, :], emb_s[:, :], start=True, stop=True).then_inc(pair_table_ready, 1)
            pe.wait_ge(setup_steps, SET_TOTAL)
            pe.wait_ge(consts_ready, 16)

            def spread(c, f):
                pe.wait_ge(dst_type_ready, c + 1)
                if f >= 1:
                    pe.wait_ge(apart_ready, c)
                for t in range(C):
                    last = mm(p_type[:, t * P:(t + 1) * P], dst_type[:, t:t + 1].broadcast_to([P, P]), ident[:, :],
                              start=True, stop=True)
                last.then_inc(dst_type_spread, 1)

            def layer1(c, f):
                pe.wait_ge(src_in[f % RING], nth(c, f, RING, 32))
                if f >= 1:
                    pe.wait_ge(hidden_ready, c)
                pe.sem_inc(pe_count, 1)
                mm(p_hid[0:A * H, 0:B * P], w1s, att[f % RING], start=True, stop=True).then_inc(layer1_ready, 1)

            def pairs(c, f):
                pe.wait_ge(onehot_ready, c + 1)
                if f >= 1:
                    pe.wait_ge(adapt_ready, c)
                for t in range(C):
                    for n in range(3):
                        last = mm(p_pair[:, t * NZ:(t + 1) * NZ], onehot[0:NZ, t * P:(t + 1) * P], pair[n],
                                  start=(n == 0), stop=(n == 2))
                last.then_inc(pair_rows_ready, 1)

            def layer2(c, f):
                pe.wait_ge(hidden_ready, c + 1)
                if f >= 1:
                    pe.wait_ge(gates_ready, c)
                for b in range(B):
                    last = mm(p_gate[:, b * A * H:(b + 1) * A * H], hid[:, b * P:(b + 1) * P], w2s,
                              start=True, stop=True)
                last.then_inc(layer2_ready, 1)

            def lookup(c, f):
                pe.wait_ge(compared, c + 1)
                for g in range(2):
                    if f >= 1:
                        pe.wait_ge(src_type_found, 2 * c - (1 - g))
                    for b in range(2):
                        t = 2 * g + b
                        for k in range(ZK):
                            last = mm(p_look[g][:, b * ZW:(b + 1) * ZW], above[f % 2][:, k, t * P:(t + 1) * P],
                                      zdiff[:, k, :], start=(k == 0), stop=(k == ZK - 1))
                    last.then_inc(looked_up, 1)

            def group(c, f):
                pe.wait_ge(messages_ready, c + 1)
                if f >= 1:
                    pe.wait_ge(grouped_in_sbuf, c)
                mk = mask[f % 2]
                for g in range(2):
                    o = g * 3 * P
                    t = 2 * g
                    mm(p_group[:, t * S:(t + 1) * S], mk[:, o:o + P], centred[:, t, :], start=True, stop=False)
                    mm(p_group[:, t * S:(t + 1) * S], mk[:, o + P:o + 2 * P], centred[:, t + 1, :], start=False, stop=True)
                    last = mm(p_group[:, (t + 1) * S:(t + 2) * S], mk[:, o + 2 * P:o + 3 * P], centred[:, t + 1, :],
                              start=True, stop=True)
                last.then_inc(grouped, 1)

            def turn(c, f, more=True):
                if more:
                    spread(c + 1, f + 1)
                    layer1(c + 1, f + 1)
                if f >= 1:
                    group(c - 1, f - 1)
                if more:
                    pairs(c + 1, f + 1)
                    layer2(c + 1, f + 1)
                    lookup(c + 1, f + 1)

            spread(0, 0)
            layer1(0, 0)
            pairs(0, 0)
            layer2(0, 0)
            lookup(0, 0)
            chunks(pe, turn, PEEL - 1, NCH - 1)
            turn(NCH - 1, NCH - 1, more=False)
            group(NCH - 1, NCH - 1)

            def turn_t(n, f, on):
                if not on(4):
                    return
                k, q, h = n - 4, (f - 4) % TRING, (f - 4) % 2
                pe.wait_ge(stored[q], nth(k, f - 4, TRING, 16))
                pe.sem_inc(pe_count, 1)
                for a, b in SPLIT:
                    mm(row_out(q, a, b), ones[:, :], beta_parts[:, :, :].broadcast_to([BK, b - a, H]), start=True, stop=False)
                    mm(row_out(q, a, b), identf[:, :], xc[:, bass.ds(k * CJ + a, b - a), :], start=False, stop=False)
                pe.wait_ge(scaled_ready, k + 1)
                pe.sem_inc(pe_count, 1)
                for a, b in SPLIT:
                    last = mm(row_out(q, a, b), identf[:, :], y_t[q][:, a:b, :], start=False, stop=False)
                last.then_inc(scaled_added, 1)
                pe.wait_ge(scaled_sums_ready, k + 1)
                pe.sem_inc(pe_count, 1)
                for a, b in SPLIT:
                    last = mm(row_out(q, a, b), mean_w[:, :], scaled_sums[h][:, a:b, :].broadcast_to([P, b - a, H]),
                              start=False, stop=True)
                last.then_inc(centred_ready, 1)

            turns(pe, turn_t)




def kernel(x, src, dst, edge_attr_40, edge_weight, node_type_119, node_vec, L0_gnn_W1, L0_gnn_b1, L0_gnn_W2, L0_gnn_b2,
           L0_gnn_emb, L0_gnn_adaptW, L0_gnn_gamma, L0_gnn_beta):
    import numpy as np
    import concourse.bacc as bacc
    from concourse.bass_utils import run_bass_kernel_spmd

    def padded(a, fill):
        rows = np.full((EPAD - E,) + a.shape[1:], fill, a.dtype)
        return np.concatenate([np.asarray(a), rows])

    x = np.asarray(x)
    table = np.empty((N, W), np.float32)
    table[:, 0:H] = x
    table[:, H] = np.asarray(node_vec)
    table.view(np.int32)[:, H + 1] = np.asarray(node_type_119)
    src_p = padded(src, PAD_ROW)
    dst_p = padded(dst, 0)
    z = np.concatenate([np.asarray(node_type_119), np.zeros(ZR * ZW - N, node_type_119.dtype)]).reshape(ZR, ZW)
    z_before = np.roll(z, 1, axis=0)
    w1 = np.zeros((A * R_ATTR, A * H), np.float32)
    w2 = np.zeros((A * H + 1, A * H), np.float32)
    for a in range(A):
        w1[a * R_ATTR:(a + 1) * R_ATTR, a * H:(a + 1) * H] = np.asarray(L0_gnn_W1).T
        w2[a * H:(a + 1) * H, a * H:(a + 1) * H] = np.asarray(L0_gnn_W2).T
        w2[A * H, a * H:(a + 1) * H] = np.asarray(L0_gnn_b2)
    arrays = {
        "in_x": x,
        "in_table": table,
        "in_src_row": src_p.reshape(NCH, EC),
        "in_cols": dst_p.reshape(NCH, C, P).transpose(0, 2, 1),
        "in_src_col": src_p.reshape(NT, P).T,
        "in_weight": padded(edge_weight, 0).reshape(NT, P).T,
        "in_attr": padded(edge_attr_40, 0).reshape(NCH, B, A, P, R_ATTR).transpose(0, 2, 4, 1, 3).reshape(
            NCH, A * R_ATTR, B * P),
        "in_z_rows": z.reshape(ZK, P, ZW).transpose(1, 0, 2),
        "in_z_before": z_before.reshape(ZK, P, ZW).transpose(1, 0, 2),
        "in_w1": w1,
        "in_b1": np.tile(np.asarray(L0_gnn_b1), A).reshape(A * H, 1),
        "in_w2": w2,
        "in_emb_t": np.asarray(L0_gnn_emb).T,
        "in_adapt_t": np.asarray(L0_gnn_adaptW).T,
        "in_gamma": np.asarray(L0_gnn_gamma).reshape(1, H),
        "in_beta": np.asarray(L0_gnn_beta).reshape(1, H),
    }
    arrays = {k: np.ascontiguousarray(a) for k, a in arrays.items()}
    nc = bacc.Bacc("TRN2", target_bir_lowering=False, num_devices=1)
    args = [nc.dram_tensor(k, a.shape, mybir.dt.from_np(a.dtype), kind="ExternalInput").ap() for k, a in arrays.items()]
    out = nc.dram_tensor("out", (N, H), F32, kind="ExternalOutput").ap()
    gnn_resnorm(nc, *args, out)
    r = run_bass_kernel_spmd(nc, [arrays], core_ids=[0])
    return r.results[0]["out"]
```
